# Optimizing a Trainium2 kernel written in Bass

```python
import numpy as np
import jax
import jax.numpy as jnp

def _softmax(x, axis=-1):
    return jax.nn.softmax(x, axis=axis)

def _gelu(x):
    return jax.nn.gelu(x, approximate=True)

def _silu(x):
    return jax.nn.silu(x)

def _sigmoid(x):
    return jax.nn.sigmoid(x)

def _layernorm(x, axis=-1, eps=1e-05):
    m = jnp.mean(x, axis=axis, keepdims=True)
    v = jnp.var(x, axis=axis, keepdims=True)
    return (x - m) / jnp.sqrt(v + eps)

def _scatter_add(tgt, idx, src, axis=0):
    return tgt.at[idx].add(src)

def _segment_sum(src, seg, n):
    return jax.ops.segment_sum(src, seg, n)
kernel_name = 'mk_adaln_d1_jaxref_r8_37b329'

def setup_inputs(seed: int=0):
    np.random.seed(seed)
    _w = jnp.asarray

    def _L0_attn_setup():
        import jax, jax.numpy as jnp
        import numpy as np
        import math
        H = 16
        N_EMBD = 128
        EPS = 1e-05
        key = jax.random.key(seed)
        ks = jax.random.split(key, 6)
        B, T, C = (2, 256, 128)
        x = jax.random.normal(ks[0], (B, T, C), dtype=jnp.float32)
        s = 0.02
        Wq = jax.random.normal(ks[1], (C, N_EMBD), dtype=jnp.float32) * s
        Wk = jax.random.normal(ks[2], (C, N_EMBD), dtype=jnp.float32) * s
        Wv = jax.random.normal(ks[3], (C, N_EMBD), dtype=jnp.float32) * s
        Wo = jax.random.normal(ks[4], (N_EMBD, C), dtype=jnp.float32) * s
        return {'x': x, 'Wq': Wq, 'bq': jnp.zeros((N_EMBD,), jnp.float32), 'Wk': Wk, 'bk': jnp.zeros((N_EMBD,), jnp.float32), 'Wv': Wv, 'bv': jnp.zeros((N_EMBD,), jnp.float32), 'Wo': Wo, 'bo': jnp.zeros((C,), jnp.float32), 'gamma': jnp.ones((C,), jnp.float32), 'beta': jnp.zeros((C,), jnp.float32)}
    _L0_attn_in = _L0_attn_setup()

    def _L0_ffn_setup():
        import jax, jax.numpy as jnp
        import numpy as np
        TOP_K = 2
        NUM_EXPERTS = 8
        key = jax.random.key(seed)
        ks = jax.random.split(key, 8)
        h, d, ds, E = (128, 64, 128, NUM_EXPERTS)
        s = 1.0 / np.sqrt(h)
        return {'x': jax.random.normal(ks[0], (2, 256, h), jnp.float32), 'router': jax.random.normal(ks[1], (h, E), jnp.float32) * s, 'experts_gate': jax.random.normal(ks[2], (E, h, d), jnp.float32) * s, 'experts_up': jax.random.normal(ks[3], (E, h, d), jnp.float32) * s, 'experts_down': jax.random.normal(ks[4], (E, d, h), jnp.float32) * (1.0 / np.sqrt(d)), 'shared_gate': jax.random.normal(ks[5], (h, ds), jnp.float32) * s, 'shared_up': jax.random.normal(ks[6], (h, ds), jnp.float32) * s, 'shared_down': jax.random.normal(ks[7], (ds, h), jnp.float32) * (1.0 / np.sqrt(ds))}
    _L0_ffn_in = _L0_ffn_setup()
    _L0_c = _w((lambda *s: np.random.randn(*s).astype(np.float32) * 0.05)(8, 128))
    _L0_wmod = _w((lambda *s: np.random.randn(*s).astype(np.float32) * 0.05)(128, 6 * 128) * 128 ** (-0.5))
    _d = {'L0_attn_x': _L0_attn_in['x'], 'L0_attn_Wq': _L0_attn_in['Wq'], 'L0_attn_bq': _L0_attn_in['bq'], 'L0_attn_Wk': _L0_attn_in['Wk'], 'L0_attn_bk': _L0_attn_in['bk'], 'L0_attn_Wv': _L0_attn_in['Wv'], 'L0_attn_bv': _L0_attn_in['bv'], 'L0_attn_Wo': _L0_attn_in['Wo'], 'L0_attn_bo': _L0_attn_in['bo'], 'L0_attn_gamma': _L0_attn_in['gamma'], 'L0_attn_beta': _L0_attn_in['beta'], 'L0_ffn_router': _L0_ffn_in['router'], 'L0_ffn_experts_gate': _L0_ffn_in['experts_gate'], 'L0_ffn_experts_up': _L0_ffn_in['experts_up'], 'L0_ffn_experts_down': _L0_ffn_in['experts_down'], 'L0_ffn_shared_gate': _L0_ffn_in['shared_gate'], 'L0_ffn_shared_up': _L0_ffn_in['shared_up'], 'L0_ffn_shared_down': _L0_ffn_in['shared_down'], 'L0_c': _L0_c, 'L0_wmod': _L0_wmod}
    _x0 = _d['L0_attn_x']
    _d['L0_attn_x'] = jax.random.normal(jax.random.fold_in(jax.random.key(seed), 1), (8, 512, 128), dtype=_x0.dtype)
    del _x0
    return _d

def reference(L0_attn_x, L0_attn_Wq, L0_attn_bq, L0_attn_Wk, L0_attn_bk, L0_attn_Wv, L0_attn_bv, L0_attn_Wo, L0_attn_bo, L0_attn_gamma, L0_attn_beta, L0_ffn_router, L0_ffn_experts_gate, L0_ffn_experts_up, L0_ffn_experts_down, L0_ffn_shared_gate, L0_ffn_shared_up, L0_ffn_shared_down, L0_c, L0_wmod):

    def _L0_attn_ref(x, Wq, bq, Wk, bk, Wv, bv, Wo, bo, gamma, beta):
        import jax, jax.numpy as jnp
        import numpy as np
        import math
        H = 16
        N_EMBD = 128
        EPS = 1e-05
        B, T, _ = x.shape
        Dh = N_EMBD // H

        def split_heads(y):
            return y.reshape(B, T, H, Dh).transpose(0, 2, 1, 3)
        q = split_heads(x @ Wq + bq)
        k = split_heads(x @ Wk + bk)
        v = split_heads(x @ Wv + bv)
        att = jnp.einsum('bhtd,bhsd->bhts', q, k) * (1.0 / math.sqrt(Dh))
        causal = jnp.tril(jnp.ones((T, T), dtype=bool))
        att = jnp.where(causal[None, None], att, -jnp.inf)
        att = jax.nn.softmax(att, axis=-1)
        o = jnp.einsum('bhts,bhsd->bhtd', att, v)
        o = o.transpose(0, 2, 1, 3).reshape(B, T, N_EMBD)
        y = o @ Wo + bo
        mu = jnp.mean(y, axis=-1, keepdims=True)
        var = jnp.var(y, axis=-1, keepdims=True)
        return (y - mu) * jax.lax.rsqrt(var + EPS) * gamma + beta

    def _L0_ffn_ref(x, router, experts_gate, experts_up, experts_down, shared_gate, shared_up, shared_down):
        import jax, jax.numpy as jnp
        import numpy as np
        TOP_K = 2
        NUM_EXPERTS = 8
        b, s, h = x.shape
        E = router.shape[1]
        shared_act = jax.nn.silu(jnp.einsum('bsh,hd->bsd', x, shared_gate))
        shared_up_out = jnp.einsum('bsh,hd->bsd', x, shared_up)
        shared_out = jnp.einsum('bsd,dh->bsh', shared_act * shared_up_out, shared_down)
        router_probs = jax.nn.softmax(jnp.einsum('bsh,he->bse', x, router), axis=-1)
        topk_probs, topk_idx = jax.lax.top_k(router_probs, TOP_K)
        coef = jnp.sum(jax.nn.one_hot(topk_idx, E, dtype=x.dtype) * topk_probs[..., None], axis=2)
        coef = coef.reshape(b * s, E)
        x_flat = x.reshape(b * s, h)
        gate = jnp.einsum('th,ehd->etd', x_flat, experts_gate)
        up = jnp.einsum('th,ehd->etd', x_flat, experts_up)
        expert_out = jnp.einsum('etd,edh->eth', jax.nn.silu(gate) * up, experts_down)
        routed = jnp.einsum('eth,te->th', expert_out, coef)
        return routed.reshape(b, s, h) + shared_out
    x = L0_attn_x
    mod = (_silu(L0_c) @ L0_wmod).reshape(L0_c.shape[0], 6, 1, -1)
    sa, ca, ga, sb, cb, gb = (mod[:, 0], mod[:, 1], mod[:, 2], mod[:, 3], mod[:, 4], mod[:, 5])
    ga = (2 * (ga >= 0) - 1) * jnp.maximum(jnp.abs(ga), 0.25)
    gb = (2 * (gb >= 0) - 1) * jnp.maximum(jnp.abs(gb), 0.25)
    h = _layernorm(x, axis=-1) * (1 + ca) + sa
    x = x + ga * _L0_attn_ref(h, L0_attn_Wq, L0_attn_bq, L0_attn_Wk, L0_attn_bk, L0_attn_Wv, L0_attn_bv, L0_attn_Wo, L0_attn_bo, L0_attn_gamma, L0_attn_beta)
    h = _layernorm(x, axis=-1) * (1 + cb) + sb
    x = x + gb * _L0_ffn_ref(h, L0_ffn_router, L0_ffn_experts_gate, L0_ffn_experts_up, L0_ffn_experts_down, L0_ffn_shared_gate, L0_ffn_shared_up, L0_ffn_shared_down)
    return x

_drawn_inputs = setup_inputs


def setup_inputs(seed=0):
    import zlib

    import numpy as np

    out = dict(_drawn_inputs(seed))
    spreads = {'L0_attn_bq': (0.0, 0.8),
     'L0_attn_bk': (0.0, 0.8),
     'L0_attn_bv': (0.0, 0.1),
     'L0_attn_bo': (0.0, 0.1),
     'L0_attn_gamma': (1.0, 0.2),
     'L0_attn_beta': (0.0, 0.359)}
    factors = {'L0_attn_Wq': 8.0, 'L0_attn_Wk': 8.0, 'L0_attn_Wv': 3.871}
    for name, (base, spread) in spreads.items():
        noise = np.random.default_rng([zlib.crc32(name.encode()), seed]).standard_normal(out[name].shape)
        drawn = base * np.exp(spread * noise) if base else spread * noise
        out[name] = jnp.asarray(drawn.astype(out[name].dtype))
    for name, factor in factors.items():
        out[name] = (out[name] * factor).astype(out[name].dtype)
    return out
```

```python
from contextlib import ExitStack

import concourse.bass as bass
from concourse import mybir

F32 = mybir.dt.float32
BF16 = mybir.dt.bfloat16
ALU = mybir.AluOpType
ACT = mybir.ActivationFunctionType
AX_X = mybir.AxisListType.X

P = 128
B = 8
T = 512
TT = T // P
C = 128
H = 16
DH = C // H
GH = 4
G = H // GH
NG = B * G
PARTS = 3
KROWS = PARTS * PARTS * DH
MROWS = KROWS + PARTS
SROWS = PARTS * DH
E = 8
DE = 64
FB = E * DE // P
MB = FB + 1
VC = 32
EPS = 1e-5
SCALE = DH ** -0.5
MASKED = -3.0e38

S1_UNITS = ([(h, 1, 3) for h in range(GH)] + [(h, 1, 2) for h in range(GH)]
            + [(0, 2, 1), (2, 2, 1)] + [(0, 4, 0)])
S2_UNITS = ([[(h, 0)] for h in range(GH)] + [[(h, 1), (h, 3)] for h in range(GH)]
            + [[(0, 2), (1, 2)], [(2, 2), (3, 2)]])
U1, U2 = len(S1_UNITS), len(S2_UNITS)
P_AT = {0: 0, 1: 512, 3: 896, 2: 1024}
P_LEN = 1280
PV_ORDER = [(0, 4), (1, 8), (3, 8), (2, 10)]

EXTRA = {
    0: {0: [("xres", "prev"), ("xin", "next")], 1: [("o", "")]},
    1: {0: [("vaug", "cur")], 1: [("o", "")], 2: [("ot", "prev")], 3: [("y", "prev")],
        5: [("yn", "prev")], 6: [("x2", "prev")], 8: [("x2n", "prev")], 9: [("xs", "next")],
        10: [("x2t", "prev")], 11: [("xn", "next")]},
    2: {0: [("lg", "prev"), ("route", "prev")], 1: [("o", ""), ("xt", "next")], 2: [("q", "next")],
        3: [("rank", "prev")], 4: [("k", "next")], 6: [("v", "next"), ("stack", "next")],
        7: [("ct", "prev")], 8: [("g0", "prev")], 9: [("u0", "prev")], 10: [("c0", "prev")],
        11: [("g1", "prev")], 12: [("u1", "prev"), ("c1", "prev")]},
    3: {1: [("o", "")], 2: [("g2", "prev")], 3: [("u2", "prev"), ("c2", "prev")],
        5: [("g3", "prev")], 6: [("u3", "prev"), ("c3", "prev")],
        8: [("g4", "prev")], 9: [("u4", "prev")], 11: [("down", "prev")]},
}


def slots(has_prev, has_cur, has_next):
    live = {"prev": has_prev, "cur": has_cur, "next": has_next}
    out = []
    for s in range(G):
        s1 = has_cur
        s2 = has_cur and (s > 0 or has_prev) or (has_prev and s == 0)
        o = (has_prev and s < 2) or (has_cur and s >= 2)
        for k in range(U1 + 2):
            if s1 and k == 0:
                out.append((s, "load", 0))
            if s1 and k < U1:
                out.append((s, "s1", k))
            if s2 and 0 <= k - 3 < U2:
                out.append((s, "s2", k - 3))
            for name, whose in EXTRA[s].get(k, []):
                if (name == "o" and o) or (name != "o" and live[whose]):
                    out.append((s, name, 0) if name[-1] not in "01234" or name == "x2"
                               else (s, name[0], int(name[1])))
        if s2:
            out += [(s, "pv", 0), (s, "pv", 1)]
        if s1:
            out.append((s, "max", 0))
        if s2:
            out += [(s, "pv", 2), (s, "pv", 3), (s, "uev", 0)]
    return out


PROLOGUE = [(0, t, 0) for t in ("xin", "xs", "xn", "xt", "q", "k", "v", "stack", "first")]
KINDS = {-1: PROLOGUE, 0: slots(False, True, True), 1: slots(True, True, True),
         7: slots(True, True, False), 8: slots(True, False, False)}
LOOP = (1, 7)

MISC_TASKS = ("o", "ot", "y", "x2t", "lg", "ct", "c", "xt", "q", "k", "v", "max")


def misc_uses(kind):
    return [x for x in KINDS[kind] if x[1] in MISC_TASKS]


def misc_at(it, task):
    before = len(misc_uses(-1))
    if isinstance(it, int) and it <= 0:
        return (before if it == 0 else 0) + misc_uses(it).index(task)
    before += len(misc_uses(0))
    each = len(misc_uses(1))
    if isinstance(it, int) and it >= LOOP[1]:
        before += (LOOP[1] - 1) * each + (len(misc_uses(7)) if it == 8 else 0)
        return before + misc_uses(it).index(task)
    return it * each + (before - each + misc_uses(1).index(task))


def need(eng, sem, value):
    if not isinstance(value, int) or value > 0:
        eng.wait_ge(sem, value)


def need_all(eng, const, *waits):
    waits = [(m, v if isinstance(v, int) else eng.to_reg(v)) for m, v in waits]
    eng.wait_ge(*const)
    for m, v in waits:
        need(eng, m, v)


def walk(eng, run):
    for it in (-1, 0):
        for s, name, a in KINDS[it]:
            run(it, s, name, a)
    with eng.Fori(*LOOP) as it:
        for s, name, a in KINDS[1]:
            run(it, s, name, a)
    for it in (7, 8):
        for s, name, a in KINDS[it]:
            run(it, s, name, a)


def block_kernel(nc, x, Wq, bq, Wk, bk, Wv, bv, Wo, bo, gamma, beta, router, w_gate, w_up, w_down,
                 sh_gate, sh_up, sh_down, cond, wmod, out):
    q_scr = nc.dram_tensor("q_scr", [P, PARTS, T], BF16, kind="Internal").ap()
    k_scr = [nc.dram_tensor(f"k_scr{r}", [P, PARTS, T], BF16, kind="Internal").ap()
             for r in range(PARTS)]

    with ExitStack() as ctx:
        def sb(name, shape, dt=F32):
            return ctx.enter_context(nc.sbuf_tensor(name, shape, dt))

        def bank(name):
            return ctx.enter_context(nc.psum_tensor(name, [P, 512], F32))

        def sem(name):
            return ctx.enter_context(nc.semaphore(name))

        s1_bank = [bank("s1_bank0"), bank("s1_bank1")]
        s2_bank = [bank("s2_bank0"), bank("s2_bank1")]
        pv_bank, misc, gate_bank, up_bank = (bank(x) for x in ("pv_bank", "misc", "gate_bank", "up_bank"))
        misc_tok = misc[:, :].rearrange("p (t c) -> p t c", t=TT)
        misc_bf = misc[:, :].bitcast(BF16)

        wq, wk, wv, wo = (sb(x, [P, C]) for x in ("wq", "wk", "wv", "wo"))
        wg, wu = sb("wg", [P, MB * P]), sb("wu", [P, MB * P])
        wd = sb("wd", [P, MB, C])
        w_router = sb("w_router", [P, P])
        bq_col, bk_col = sb("bq_col", [P, 1]), sb("bk_col", [P, 1])
        bv_row, bo_row, gamma_row, beta_row = (sb(x, [P, C]) for x in ("bv_row", "bo_row", "gamma_row", "beta_row"))
        wmod_sb = sb("wmod_sb", [P, 6 * C])
        cond_sb, cond_t, cond_s = (sb(x, [B, P]) for x in ("cond_sb", "cond_t", "cond_s"))
        cond_T = sb("cond_T", [P, B])
        cond_rep = sb("cond_rep", [P, B, P])
        mod_cols = sb("mod_cols", [P, 4, B])
        gate_a, gate_b = sb("gate_a", [P, B, C]), sb("gate_b", [P, B, C])
        gate_sign, gate_abs = sb("gate_sign", [P, B, C]), sb("gate_abs", [P, B, C])
        gamma_a, beta_a = sb("gamma_a", [P, B, C]), sb("beta_a", [P, B, C])
        ident, ident_bf = sb("ident", [P, P]), sb("ident_bf", [P, P], BF16)
        causal = sb("causal", [P, P], BF16)
        pick = sb("pick", [P, FB, 2, DE], BF16)
        earlier = sb("earlier", [P, E, E])
        neg_half = sb("neg_half", [P, TT])
        x_in, x_n = sb("x_in", [P, TT, C]), sb("x_n", [P, TT, C])
        h1T = sb("h1T", [P, T])
        q_parts, k_parts = sb("q_parts", [P, PARTS, T], BF16), sb("k_parts", [P, PARTS, T], BF16)
        q_rest, k_rest = sb("q_rest", [P, T]), sb("k_rest", [P, T])
        v_tok = sb("v_tok", [P, TT, C])
        q_stack, k_stack = sb("q_stack", [P, H, T], BF16), sb("k_stack", [P, H, T], BF16)
        v_aug = sb("v_aug", [P, TT, H, VC])
        row_max = [sb(f"row_max{i}", [P, GH, TT]) for i in range(2)]
        max_parts = sb("max_parts", [P, PARTS, GH * TT], BF16)
        max_rest = sb("max_rest", [P, GH * TT])
        max_rows = sb("max_rows", [PARTS * GH * TT, P], BF16)
        probs = [sb(f"probs{i}", [P, GH, P_LEN]) for i in range(2)]
        u_sb = sb("u_sb", [P, T])
        denom = sb("denom", [P, TT * GH])
        o_tok = sb("o_tok", [P, TT, C])
        oT = sb("oT", [P, T])
        x_res, y_sb, x2, x2_n = (sb(x, [P, TT, C]) for x in ("x_res", "y_sb", "x2", "x2_n"))
        h2T = sb("h2T", [P, T])
        stats = {k: sb(f"stats_{k}", [P, TT, 6]) for k in ("x", "y", "x2")}
        mean_var = {k: sb(f"mean_var_{k}", [P, TT, 2]) for k in ("x", "y", "x2")}
        var_eps = {k: sb(f"var_eps_{k}", [P, TT]) for k in ("x", "y", "x2")}
        rstd = {k: sb(f"rstd_{k}", [P, TT]) for k in ("x", "y", "x2")}
        lmax, esum, erec = (sb(x, [P, TT]) for x in ("lmax", "esum", "erec"))
        logit, expo, prob, rank, coef, coef_rest = (
            sb(x, [P, TT, E]) for x in ("logit", "expo", "prob", "rank", "coef", "coef_rest"))
        above, equal = sb("above", [P, TT, E, E]), sb("equal", [P, TT, E, E])
        coef_parts = sb("coef_parts", [P, TT, P], BF16)
        coef_T = sb("coef_T", [P, T], BF16)
        tanh_sb, silu_sb = sb("tanh_sb", [P, T]), sb("silu_sb", [P, T])
        hidden = sb("hidden", [P, MB, T])
        ffn_sb, out_sb = sb("ffn_sb", [P, TT, C]), sb("out_sb", [P, TT, C])

        w_in = sem("w_in")
        cond_in = sem("cond_in")
        const_step = sem("const_step")
        const_done = sem("const_done")
        ct_step = sem("ct_step")
        cond_mm = sem("cond_mm")
        gates_read = sem("gates_read")
        vec_setup = sem("vec_setup")
        x_in_ready, x_stats, x_mv = sem("x_in_ready"), sem("x_stats"), sem("x_mv")
        x_ve, x_rstd, x_norm = sem("x_ve"), sem("x_rstd"), sem("x_norm")
        q_first, k_first = sem("q_first"), sem("k_first")
        q_second, k_second, q_split, k_split = (sem(x) for x in ("q_second", "k_second", "q_split", "k_split"))
        scr_written = sem("scr_written")
        misc_written, misc_read = sem("misc_written"), sem("misc_read")
        stacked = [sem(f"stacked{g}") for g in range(G)]
        s1_written, s1_reduced = sem("s1_written"), sem("s1_reduced")
        s2_written, exp_done, probs_ready = sem("s2_written"), sem("exp_done"), sem("probs_ready")
        max_step, max_split, max_landed = sem("max_step"), sem("max_split"), sem("max_landed")
        pv_done, u_ready, denom_ready, v_ready = (sem(x) for x in ("pv_done", "u_ready", "denom_ready", "v_ready"))
        xres_in, xres_ready = sem("xres_in"), sem("xres_ready")
        y_stats, y_mv, y_ve, y_rstd = (sem(x) for x in ("y_stats", "y_mv", "y_ve", "y_rstd"))
        x2_stats, x2_mv, x2_ve, x2_rstd, x2_norm = (
            sem(x) for x in ("x2_stats", "x2_mv", "x2_ve", "x2_rstd", "x2_norm"))
        y_norm, y_scaled, x2_ready = sem("y_norm"), sem("y_scaled"), sem("x2_ready")
        lmax_ready, logit_ready, expo_ready = sem("lmax_ready"), sem("logit_ready"), sem("expo_ready")
        route_step, coef_ready, coef_step, coef_split = (
            sem(x) for x in ("route_step", "coef_ready", "coef_step", "coef_split"))
        gate_written, tanh_ready, gate_read = sem("gate_written"), sem("tanh_ready"), sem("gate_read")
        up_written, up_read = sem("up_written"), sem("up_read")
        down_written, ffn_gated, out_ready, stored = (
            sem(x) for x in ("down_written", "ffn_gated", "out_ready", "stored"))
        block = ctx.enter_context(nc.Block())

        N_WEIGHTS = 20
        Q_DMAS = 2 * PARTS
        SCR_DMAS = 1 + 1 + 2 * (PARTS - 1)
        GATE_USES = MB + 1
        ROUTE_STEPS = 8

        def tok(dram, b):
            return dram[b].rearrange("(t p) c -> p t c", p=P)

        def over_tiles(row):
            return row.unsqueeze(1).to_broadcast([P, TT, C])

        @block.sync
        def _(sp):
            sp.dma_start(cond_sb[:, :], cond).then_inc(cond_in, 16)
            sp.dma_start(wmod_sb[:, :], wmod).then_inc(cond_in, 16)
            sp.dma_start(x_in[:, :, :], tok(x, 0)).then_inc(x_in_ready, 16)
            for dst, src in ((wq, Wq), (wk, Wk), (wv, Wv), (wo, Wo)):
                sp.dma_start(dst[:, :], src).then_inc(w_in, 16)
            sp.dma_start(bq_col[:, :], bq.unsqueeze(1)).then_inc(w_in, 16)
            sp.dma_start(bk_col[:, :], bk.unsqueeze(1)).then_inc(w_in, 16)
            for dst, src in ((bv_row, bv), (bo_row, bo), (gamma_row, gamma), (beta_row, beta)):
                sp.dma_start(dst[:, :], src.unsqueeze(0).to_broadcast([P, C])).then_inc(w_in, 16)
            sp.wait_ge(const_done, 1)
            sp.dma_start(w_router[:, 0:E], router).then_inc(w_in, 16)
            for dst, experts, shared in ((wg, w_gate, sh_gate), (wu, w_up, sh_up)):
                sp.dma_start(dst[:, 0:FB * P].rearrange("p (e d) -> p e d", e=E),
                             experts.rearrange("e h d -> h e d")).then_inc(w_in, 16)
                sp.dma_start(dst[:, FB * P:MB * P], shared).then_inc(w_in, 16)
            for m in range(FB):
                sp.dma_start(wd[:, m, :], w_down[2 * m:2 * m + 2].rearrange("e d h -> (e d) h")).then_inc(w_in, 16)
            sp.dma_start(wd[:, FB, :], sh_down).then_inc(w_in, 16)

            def load_stacks(it, g):
                need(sp, s2_written, it * (G * U2) + U2 * (g + 1 - G))
                need(sp, scr_written, it * (16 * SCR_DMAS) + 16 * SCR_DMAS)
                heads = slice(GH * g, GH * g + GH)
                for r in range(PARTS):
                    rows = slice(SROWS * r, SROWS * (r + 1))
                    for stack, scr in ((q_stack, q_scr), (k_stack, k_scr[r])):
                        src = scr.rearrange("(h d) s t -> (d s) h t", d=DH)
                        sp.dma_start(stack[rows, heads, :], src[:, heads, :]).then_inc(stacked[g], 16)

            def run(it, s, name, a):
                if name == "xin" and not (isinstance(it, int) and it == -1):
                    need(sp, x_norm, it + 1)
                    sp.dma_start(x_in[:, :, :], tok(x, it + 1)).then_inc(x_in_ready, 16)
                if name == "xres":
                    need(sp, x2_ready, it - 1)
                    sp.dma_start(x_res[:, :, :], tok(x, it - 1)).then_inc(xres_in, 16)
                if name == "stack":
                    sp.wait_ge(const_done, 1)
                    for g in range(G):
                        need(sp, stacked[g], it * (16 * Q_DMAS) + 16 * Q_DMAS)
                    sp.wait_ge(q_split, it + 2)
                    sp.dma_start(q_scr, q_parts[:, :, :]).then_inc(scr_written, 16)
                    sp.wait_ge(k_split, it + 2)
                    sp.dma_start(k_scr[0], k_parts[:, :, :]).then_inc(scr_written, 16)
                    for r in range(1, PARTS):
                        sp.dma_start(k_scr[r][:, 0:PARTS - r, :], k_parts[:, r:PARTS, :]).then_inc(scr_written, 16)
                        sp.dma_start(k_scr[r][:, PARTS - r:PARTS, :], k_parts[:, 0:r, :]).then_inc(scr_written, 16)
                if name == "first":
                    sp.wait_ge(const_step, 2)
                    load_stacks(0, 0)
                    load_stacks(0, 1)
                if name == "load" and s < 2:
                    load_stacks(it, s + 2)
                if name == "max" and s >= 2 and has_next(it):
                    load_stacks(it + 1, s - 2)
                if name == "down":
                    sp.wait_ge(out_ready, it)
                    sp.dma_start(tok(out, it - 1), out_sb[:, :, :]).then_inc(stored, 16)

            def has_next(it):
                return not isinstance(it, int) or it < B - 1

            walk(sp, run)
            sp.wait_ge(stored, 16 * B)

        @block.gpsimd
        def _(pool):
            nc.gpsimd.memset(w_router[:, :], 0.0).then_inc(const_done, 1)
            nc.gpsimd.memset(neg_half[:, :], -0.5)
            nc.gpsimd.memset(ident[:, :], 0.0)
            nc.gpsimd.memset(ident_bf[:, :], 0.0).then_inc(const_step, 1)
            pool.wait_ge(const_step, 1)
            nc.gpsimd.affine_select(out=ident[:, :], in_=ident[:, :], compare_op=ALU.not_equal, fill=1.0,
                                    base=0, pattern=[[-1, P]], channel_multiplier=1)
            nc.gpsimd.affine_select(out=ident_bf[:, :], in_=ident_bf[:, :], compare_op=ALU.not_equal, fill=1.0,
                                    base=0, pattern=[[-1, P]], channel_multiplier=1).then_inc(const_done, 1)
            pool.wait_ge(const_done, 2)
            nc.gpsimd.memset(k_stack[64:MROWS, :, :], -1.0).then_inc(const_step, 1)
            pool.wait_ge(const_step, 2)
            nc.gpsimd.memset(causal[:, :], 0.0)
            nc.gpsimd.memset(pick[:, :, :, :], 0.0)
            nc.gpsimd.memset(earlier[:, :, :], 1.0)
            nc.gpsimd.memset(coef_parts[:, :, :], 0.0)
            nc.gpsimd.memset(v_aug[:, :, :, :], 0.0).then_inc(const_step, 1)
            pool.wait_ge(const_step, 3)
            nc.gpsimd.memset(v_aug[:, :, :, DH:DH + 1], 1.0)
            nc.gpsimd.affine_select(out=causal[:, :], in_=causal[:, :], compare_op=ALU.is_ge, fill=MASKED,
                                    base=0, pattern=[[-1, P]], channel_multiplier=1)
            nc.gpsimd.affine_select(out=earlier[:, :, :], in_=earlier[:, :, :], compare_op=ALU.is_ge, fill=0.0,
                                    base=-1, pattern=[[1, E], [-1, E]], channel_multiplier=0).then_inc(const_step, 1)
            for part in range(PARTS):
                pool.wait_ge(const_step, 4 + part)
                nc.gpsimd.affine_select(out=pick[:, :, :, :], in_=pick[:, :, :, :], compare_op=ALU.not_equal,
                                        fill=1.0, base=-part * E, pattern=[[-2, FB], [-1, 2], [0, DE]],
                                        channel_multiplier=1).then_inc(const_step, 1)
            pool.wait_ge(const_step, 4 + PARTS)
            nc.gpsimd.tensor_scalar(max_rest[:, :], ident[:, 0:GH * TT], 0.0, None, ALU.mult).then_inc(const_done, 1)

            def inv_std(key, mv_sem, ve_sem, rstd_sem, b1):
                need_all(pool, (const_done, 3), (mv_sem, b1))
                nc.gpsimd.tensor_scalar(var_eps[key][:, :], mean_var[key][:, :, 1], EPS, None, ALU.add).then_inc(ve_sem, 1)
                pool.wait_ge(ve_sem, b1)
                nc.gpsimd.tensor_tensor(rstd[key][:, :], var_eps[key][:, :], neg_half[:, :], ALU.pow).then_inc(rstd_sem, 1)

            def split_rest(it, name, parts, rest, second, done):
                need_all(pool, (const_done, 3), (misc_read, misc_at(it, name) + 1), (scr_written, it * (16 * SCR_DMAS) + 16 * SCR_DMAS))
                nc.gpsimd.tensor_scalar(parts[:, 1, :], rest[:, :], 1.0, None, ALU.mult).then_inc(second, 1)
                pool.wait_ge(second, it + 2)
                nc.gpsimd.tensor_tensor(parts[:, 2, :], rest[:, :], parts[:, 1, :], ALU.subtract).then_inc(done, 1)

            def run(it, s, name, a):
                if name == "xs":
                    inv_std("x", x_mv, x_ve, x_rstd, it + 2)
                if name == "q":
                    split_rest(it, (s, "q", 0), q_parts, q_rest, q_second, q_split)
                if name == "k":
                    split_rest(it, (s, "k", 0), k_parts, k_rest, k_second, k_split)
                if name == "s2":
                    ng = (s - 1) % G
                    pr = probs[ng % 2]
                    need_all(pool, (const_done, 3), (exp_done, it * (G * U2) + U2 * (s - 1) + a + 1))
                    h, j = S2_UNITS[a][0]
                    if a < 4:
                        view, pat = pr[:, h, P_AT[0]:P_AT[0] + P], [[1, P]]
                    elif a < 8:
                        at = P_AT[1]
                        step = P_AT[3] - P_AT[1]
                        view = pr[:, h, at:at + 2 * step].rearrange("p (a b) -> p a b", a=2)[:, :, 0:P]
                        pat = [[0, 2], [1, P]]
                    else:
                        view, pat = pr[:, h:h + 2, P_AT[2]:P_AT[2] + P], [[0, 2], [1, P]]
                    nc.gpsimd.affine_select(out=view, in_=view, compare_op=ALU.is_ge, fill=0.0, base=0,
                                            pattern=pat, channel_multiplier=-1).then_inc(probs_ready, 1)
                if name == "max":
                    rm = row_max[s % 2][:, :, :].rearrange("p h t -> p (h t)")
                    n4, c4 = it * (G * 3), 3 * s
                    need_all(pool, (const_done, 3), (s1_reduced, it * (G * U1) + U1 * (s + 1)), (misc_written, misc_prev_max(it, s)))
                    nc.gpsimd.tensor_scalar(max_parts[:, 0, :], rm, 1.0, None, ALU.mult).then_inc(max_step, 1)
                    pool.wait_ge(max_step, n4 + (c4 + 1))
                    nc.gpsimd.tensor_tensor(max_rest[:, :], rm, max_parts[:, 0, :], ALU.subtract).then_inc(max_step, 1)
                    need_all(pool, (const_done, 3), (max_step, n4 + (c4 + 2)))
                    nc.gpsimd.tensor_scalar(max_parts[:, 1, :], max_rest[:, :], 1.0, None, ALU.mult).then_inc(max_step, 1)
                    pool.wait_ge(max_step, n4 + (c4 + 3))
                    nc.gpsimd.tensor_tensor(max_parts[:, 2, :], max_rest[:, :], max_parts[:, 1, :],
                                            ALU.subtract).then_inc(max_split, 1)
                if name == "y":
                    inv_std("y", y_mv, y_ve, y_rstd, it)
                if name == "x2":
                    inv_std("x2", x2_mv, x2_ve, x2_rstd, it)
                if name == "ot":
                    pool.wait_ge(xres_in, it * 16)
                    pool.wait_ge(vec_setup, 1)
                    nc.gpsimd.tensor_tensor(x_res[:, :, :], x_res[:, :, :], over_tiles(beta_a[:, it - 1, :]),
                                            ALU.add).then_inc(xres_ready, 1)
                if name == "rank":
                    c = coef[:, :, :]
                    cp = [coef_parts[:, :, E * k:E * k + E] for k in range(PARTS)]
                    need_all(pool, (const_done, 3), (coef_ready, it))
                    nc.gpsimd.tensor_scalar(cp[0], c, 1.0, None, ALU.mult).then_inc(coef_step, 1)
                    pool.wait_ge(coef_step, it * 3 - 2)
                    nc.gpsimd.tensor_tensor(coef_rest[:, :, :], c, cp[0], ALU.subtract).then_inc(coef_step, 1)
                    need_all(pool, (const_done, 3), (coef_step, it * 3 - 1))
                    nc.gpsimd.tensor_scalar(cp[1], coef_rest[:, :, :], 1.0, None, ALU.mult).then_inc(coef_step, 1)
                    pool.wait_ge(coef_step, it * 3)
                    nc.gpsimd.tensor_tensor(cp[2], coef_rest[:, :, :], cp[1], ALU.subtract).then_inc(coef_split, 1)

            def misc_prev_max(it, s):
                if s > 0:
                    return misc_at(it, (s - 1, "max", 0)) + 1
                if isinstance(it, int) and it == 0:
                    return 0
                last = misc_at(it, misc_uses(1)[0] if not isinstance(it, int) else misc_uses(it)[0])
                return last

            walk(pool, run)

        @block.scalar
        def _(act):
            act.wait_ge(cond_in, 32)
            nc.scalar.activation(cond_t[:, :], cond_sb[:, :], ACT.Tanh, scale=0.5).then_inc(ct_step, 1)
            act.wait_ge(vec_setup, 1)
            act.wait_ge(w_in, 16 * N_WEIGHTS)

            def part_first(it, name, col, parts, first):
                act.wait_ge(misc_written, misc_at(it, name) + 1)
                need(act, scr_written, it * (16 * SCR_DMAS) + 16 * SCR_DMAS)
                nc.scalar.activation(parts[:, 0, :], misc[:, :], ACT.Identity, bias=col[:, 0:1]).then_inc(first, 1)

            def run(it, s, name, a):
                if name == "xt":
                    act.wait_ge(misc_written, misc_at(it, (s, "xt", 0)) + 1)
                    nc.scalar.activation(h1T[:, :], misc[:, :], ACT.Identity, scale=mod_cols[:, 1, it + 1].unsqueeze(1),
                                         bias=mod_cols[:, 0, it + 1].unsqueeze(1)).then_inc(misc_read, 1)
                if name == "q":
                    part_first(it, (s, "q", 0), bq_col, q_parts, q_first)
                if name == "k":
                    part_first(it, (s, "k", 0), bk_col, k_parts, k_first)
                if name == "v":
                    act.wait_ge(misc_written, misc_at(it, (s, "v", 0)) + 1)
                    need(act, v_ready, it + 1)
                    nc.scalar.activation(v_tok[:, :, :], misc_tok, ACT.Copy).then_inc(misc_read, 1)
                if name == "s2":
                    pr = probs[(s - 1) % G % 2]
                    u = U2 * (s - 1) + a
                    act.wait_ge(s2_written, it * (G * U2) + (u + 1))
                    h, j = S2_UNITS[a][0]
                    src = s2_bank[u % 2][:, :]
                    if a < 8:
                        at = P_AT[j]
                        dst = pr[:, h, at:at + 512]
                    else:
                        dst = pr[:, h:h + 2, P_AT[2]:P_AT[2] + 256]
                        src = src.rearrange("p (a b) -> p a b", a=2)
                    nc.scalar.activation(dst, src, ACT.Exp, scale=SCALE).then_inc(exp_done, 1)
                if name == "uev":
                    act.wait_ge(pv_done, it * G + s)
                    if not (isinstance(it, int) and (it, s) in ((0, 1),)):
                        act.wait_ge(misc_written, misc_at(it, (s, "o", 0)) + 1)
                    nc.scalar.activation(u_sb[:, :], pv_bank[:, :], ACT.Copy).then_inc(u_ready, 1)
                if name == "max":
                    k = misc_at(it, (s, "max", 0)) + 1
                    act.wait_ge(misc_written, k)
                    need(act, max_landed, it * (16 * G) + 16 * s)
                    nc.scalar.activation(max_rows[:, :], misc_bf[0:PARTS * GH * TT, 0:P], ACT.Copy).then_inc(misc_read, 1)
                    act.wait_ge(misc_read, k)
                    act.dma_start(q_stack[KROWS:MROWS, GH * s:GH * s + GH, :].rearrange("p h (b t) -> p (h b) t", t=P),
                                  max_rows[:, :]).then_inc(max_landed, 16)
                if name == "ot":
                    act.wait_ge(misc_written, misc_at(it, (s, "ot", 0)) + 1)
                    nc.scalar.activation(oT[:, :], misc[:, :], ACT.Copy).then_inc(misc_read, 1)
                if name == "x2t":
                    act.wait_ge(misc_written, misc_at(it, (s, "x2t", 0)) + 1)
                    nc.scalar.activation(h2T[:, :], misc[:, :], ACT.Identity, scale=mod_cols[:, 3, it - 1].unsqueeze(1),
                                         bias=mod_cols[:, 2, it - 1].unsqueeze(1)).then_inc(misc_read, 1)
                if name == "route":
                    act.wait_ge(logit_ready, it)
                    nc.scalar.activation(expo[:, :, :], logit[:, :, :], ACT.Exp).then_inc(expo_ready, 1)
                if name == "ct":
                    act.wait_ge(misc_written, misc_at(it, (s, "ct", 0)) + 1)
                    nc.scalar.activation(coef_T[:, :], misc_bf[:, 0:T], ACT.Copy).then_inc(misc_read, 1)
                if name == "g":
                    act.wait_ge(gate_written, it * MB + (a + 1 - MB))
                    if a > 0:
                        act.wait_ge(gate_read, it * GATE_USES + (a - GATE_USES))
                    nc.scalar.activation(tanh_sb[:, :], gate_bank[:, :], ACT.Tanh, scale=0.5).then_inc(tanh_ready, 1)

            walk(act, run)

        @block.vector
        def _(dve):
            dve.wait_ge(ct_step, 1)
            nc.vector.scalar_tensor_tensor(cond_s[:, :], cond_t[:, :], 1.0, cond_sb[:, :], ALU.add,
                                           ALU.mult).then_inc(ct_step, 1)
            dve.wait_ge(cond_mm, 1)
            nc.vector.tensor_scalar(cond_T[:, :], pv_bank[:, 0:B], 0.5, None, ALU.mult).then_inc(ct_step, 1)
            dve.wait_ge(ct_step, 3)
            nc.vector.tensor_copy(cond_rep[:, :, :], cond_T[:, :].unsqueeze(2).to_broadcast([P, B, P])).then_inc(ct_step, 1)
            dve.wait_ge(cond_mm, 2)
            nc.vector.tensor_copy(mod_cols[:, :, :], up_bank[:, 0:4 * B].rearrange("p (j b) -> p j b", j=4)).then_inc(ct_step, 1)
            dve.wait_ge(ct_step, 5)
            nc.vector.tensor_scalar(mod_cols[:, 1::2, :], mod_cols[:, 1::2, :], 1.0, None, ALU.add).then_inc(ct_step, 1)
            dve.wait_ge(cond_mm, 3)
            for i, (banks, gate) in enumerate(((s1_bank, gate_a), (s2_bank, gate_b))):
                for j in range(2):
                    last = nc.vector.tensor_copy(gate[:, 4 * j:4 * j + 4, :],
                                                 banks[j][:, :].rearrange("p (b c) -> p b c", b=4))
                last.then_inc(gates_read, 1)
            for i, gate in enumerate((gate_a, gate_b)):
                dve.wait_ge(gates_read, i + 1)
                dve.wait_ge(ct_step, 6 + 4 * i)
                nc.vector.tensor_scalar(gate_sign[:, :, :], gate[:, :, :], 0.0, 2.0, ALU.is_ge, ALU.mult).then_inc(ct_step, 1)
                dve.wait_ge(ct_step, 7 + 4 * i)
                nc.vector.tensor_scalar(gate_sign[:, :, :], gate_sign[:, :, :], -1.0, None, ALU.add).then_inc(ct_step, 1)
                dve.wait_ge(ct_step, 8 + 4 * i)
                nc.vector.tensor_tensor(gate_abs[:, :, :], gate[:, :, :], gate_sign[:, :, :], ALU.mult).then_inc(ct_step, 1)
                dve.wait_ge(ct_step, 9 + 4 * i)
                nc.vector.scalar_tensor_tensor(gate[:, :, :], gate_abs[:, :, :], 0.25, gate_sign[:, :, :], ALU.max,
                                               ALU.mult).then_inc(ct_step, 1)
            dve.wait_ge(w_in, 16 * N_WEIGHTS)
            dve.wait_ge(ct_step, 10)
            nc.vector.tensor_tensor(gamma_a[:, :, :], gate_a[:, :, :],
                                    gamma_row[:, :].unsqueeze(1).to_broadcast([P, B, C]), ALU.mult)
            nc.vector.tensor_tensor(beta_a[:, :, :], gate_a[:, :, :],
                                    beta_row[:, :].unsqueeze(1).to_broadcast([P, B, C]), ALU.mult).then_inc(vec_setup, 1)
            dve.wait_ge(ct_step, 14)
            dve.wait_ge(vec_setup, 1)
            dve.wait_ge(const_done, 3)

            def layer_stats(key, src, st_sem, mv_sem, b1):
                for t in range(TT):
                    last = nc.vector.bn_stats(stats[key][:, t, :], src[:, t, :])
                last.then_inc(st_sem, 1)
                need_all(dve, (const_done, 3), (st_sem, b1))
                for t in range(TT):
                    last = nc.vector.bn_aggr(mean_var[key][:, t, :], stats[key][:, t, :])
                last.then_inc(mv_sem, 1)

            def normalise(key, dst, src, rstd_sem, norm_sem, b1):
                dve.wait_ge(rstd_sem, b1)
                for t in range(TT):
                    last = nc.vector.tensor_scalar(dst[:, t, :], src[:, t, :], mean_var[key][:, t, 0:1],
                                                   rstd[key][:, t:t + 1], ALU.subtract, ALU.mult)
                last.then_inc(norm_sem, 1)

            def rest_of(it, name, col, parts, rest, first, split):
                dve.wait_ge(first, it + 2)
                need(dve, split, it + 1)
                nc.vector.scalar_tensor_tensor(rest[:, :], misc[:, :], col[:, 0:1], parts[:, 0, :], ALU.add,
                                               ALU.subtract).then_inc(misc_read, 1)

            def run(it, s, name, a):
                if name == "xs":
                    dve.wait_ge(x_in_ready, it * 16 + 32)
                    layer_stats("x", x_in, x_stats, x_mv, it + 2)
                if name == "xn":
                    normalise("x", x_n, x_in, x_rstd, x_norm, it + 2)
                if name == "q":
                    rest_of(it, name, bq_col, q_parts, q_rest, q_first, q_split)
                if name == "k":
                    rest_of(it, name, bk_col, k_parts, k_rest, k_first, k_split)
                if name == "vaug":
                    need(dve, pv_done, it * G)
                    k = misc_uses(-1) and (s, "v", 0)
                    dve.wait_ge(misc_read, v_read(it))
                    nc.vector.tensor_tensor(
                        v_aug[:, :, :, 0:DH], v_tok[:, :, :].rearrange("p t (h d) -> p t h d", h=H),
                        bv_row[:, :].rearrange("p (h d) -> p h d", h=H).unsqueeze(1).to_broadcast([P, TT, H, DH]),
                        ALU.add).then_inc(v_ready, 1)
                if name == "s1":
                    u = U1 * s + a
                    h, nh, qt = S1_UNITS[a]
                    dve.wait_ge(s1_written, it * (G * U1) + (u + 1))
                    if a == 0:
                        need(dve, max_split, it * G + (s - 1))
                    w = P * (qt + 1)
                    nc.vector.reduce_max(row_max[s % 2][:, h:h + nh, qt],
                                         s1_bank[u % 2][:, 0:nh * w].rearrange("p (h k) -> p h k", h=nh),
                                         AX_X).then_inc(s1_reduced, 1)
                if name == "o":
                    g = (s - 2) % G
                    dve.wait_ge(misc_written, misc_at(it, (s, "o", 0)) + 1)
                    if g == 0 and not (isinstance(it, int) and it == 0):
                        dve.wait_ge(misc_written, misc_at(it, (1, "ot", 0)) + 1)
                    view = misc[:, :].rearrange("p (c v) -> p c v", v=VC)
                    nc.vector.reciprocal(denom[:, :].unsqueeze(2), view[:, :, DH:DH + 1]).then_inc(denom_ready, 1)
                    dve.wait_ge(denom_ready, it * G + (s - 1))
                    nc.vector.tensor_tensor(
                        o_tok[:, :, GH * DH * g:GH * DH * (g + 1)].rearrange("p t (h d) -> p t h d", h=GH),
                        misc[:, :].rearrange("p (t h v) -> p t h v", t=TT, h=GH)[:, :, :, 0:DH],
                        denom[:, :].rearrange("p (t h) -> p t h", t=TT).unsqueeze(3).to_broadcast([P, TT, GH, DH]),
                        ALU.mult).then_inc(misc_read, 1)
                if name == "y":
                    k = misc_at(it, (s, "y", 0)) + 1
                    dve.wait_ge(misc_written, k)
                    nc.vector.tensor_tensor(y_sb[:, :, :], misc_tok, over_tiles(bo_row[:, :]), ALU.add).then_inc(misc_read, 1)
                    dve.wait_ge(misc_read, k)
                    layer_stats("y", y_sb, y_stats, y_mv, it)
                if name == "yn":
                    normalise("y", y_sb, y_sb, y_rstd, y_norm, it)
                if name == "x2":
                    dve.wait_ge(y_norm, it)
                    nc.vector.tensor_tensor(y_sb[:, :, :], y_sb[:, :, :], over_tiles(gamma_a[:, it - 1, :]),
                                            ALU.mult).then_inc(y_scaled, 1)
                    dve.wait_ge(y_scaled, it)
                    dve.wait_ge(xres_ready, it)
                    nc.vector.tensor_tensor(x2[:, :, :], y_sb[:, :, :], x_res[:, :, :], ALU.add).then_inc(x2_ready, 1)
                    dve.wait_ge(x2_ready, it)
                    layer_stats("x2", x2, x2_stats, x2_mv, it)
                if name == "x2n":
                    normalise("x2", x2_n, x2, x2_rstd, x2_norm, it)
                if name == "route":
                    dve.wait_ge(misc_written, misc_at(it, (s, "lg", 0)) + 1)
                    lg = misc_tok[:, :, 0:E]
                    nc.vector.reduce_max(lmax[:, :], lg, AX_X).then_inc(lmax_ready, 1)
                    dve.wait_ge(lmax_ready, it)
                    nc.vector.tensor_tensor(logit[:, :, :], lg, lmax[:, :].unsqueeze(2).to_broadcast([P, TT, E]),
                                            ALU.subtract).then_inc(logit_ready, 1)
                    dve.wait_ge(logit_ready, it)
                    nc.vector.tensor_scalar(lmax[:, :], lmax[:, :], 1.0, None, ALU.mult).then_inc(misc_read, 1)
                if name == "rank":
                    r0 = it * ROUTE_STEPS - ROUTE_STEPS
                    big = [P, TT, E, E]
                    dve.wait_ge(expo_ready, it)
                    nc.vector.reduce_sum(esum[:, :], expo[:, :, :], AX_X).then_inc(route_step, 1)
                    dve.wait_ge(route_step, r0 + 1)
                    nc.vector.reciprocal(erec[:, :], esum[:, :]).then_inc(route_step, 1)
                    dve.wait_ge(route_step, r0 + 2)
                    nc.vector.tensor_tensor(prob[:, :, :], expo[:, :, :], erec[:, :].unsqueeze(2).to_broadcast([P, TT, E]),
                                            ALU.mult).then_inc(route_step, 1)
                    dve.wait_ge(route_step, r0 + 3)
                    other = prob[:, :, :].unsqueeze(2).to_broadcast(big)
                    own = prob[:, :, :].unsqueeze(3).to_broadcast(big)
                    nc.vector.tensor_tensor(equal[:, :, :, :], other, own, ALU.is_equal).then_inc(route_step, 1)
                    nc.vector.tensor_tensor(above[:, :, :, :], other, own, ALU.is_gt).then_inc(route_step, 1)
                    dve.wait_ge(route_step, r0 + 4)
                    nc.vector.tensor_tensor(equal[:, :, :, :], equal[:, :, :, :],
                                            earlier[:, :, :].unsqueeze(1).to_broadcast(big), ALU.mult).then_inc(route_step, 1)
                    dve.wait_ge(route_step, r0 + 6)
                    nc.vector.tensor_tensor(above[:, :, :, :], above[:, :, :, :], equal[:, :, :, :],
                                            ALU.add).then_inc(route_step, 1)
                    dve.wait_ge(route_step, r0 + 7)
                    nc.vector.reduce_sum(rank[:, :, :], above[:, :, :, :], AX_X).then_inc(route_step, 1)
                    dve.wait_ge(route_step, r0 + 8)
                    nc.vector.scalar_tensor_tensor(coef[:, :, :], rank[:, :, :], 1.5, prob[:, :, :], ALU.is_lt,
                                                   ALU.mult).then_inc(coef_ready, 1)
                if name == "g":
                    dve.wait_ge(tanh_ready, it * MB + (a + 1 - MB))
                    nc.vector.scalar_tensor_tensor(silu_sb[:, :], tanh_sb[:, :], 1.0, gate_bank[:, :], ALU.add,
                                                   ALU.mult).then_inc(gate_read, 1)
                if name == "u":
                    dve.wait_ge(up_written, it * MB + (a + 1 - MB))
                    dve.wait_ge(gate_read, it * GATE_USES + (a + 1 - GATE_USES))
                    nc.vector.scalar_tensor_tensor(hidden[:, a, :], silu_sb[:, :], 0.5, up_bank[:, :], ALU.mult,
                                                   ALU.mult).then_inc(up_read, 1)
                if name == "c":
                    dve.wait_ge(misc_written, misc_at(it, (s, "c", a)) + 1)
                    dve.wait_ge(up_read, it * MB + (a + 1 - MB))
                    nc.vector.tensor_tensor(hidden[:, a, :], hidden[:, a, :], misc[:, :], ALU.mult).then_inc(misc_read, 1)
                if name == "down":
                    dve.wait_ge(down_written, it)
                    nc.vector.tensor_tensor(ffn_sb[:, :, :], gate_bank[:, :].rearrange("p (t c) -> p t c", t=TT),
                                            over_tiles(gate_b[:, it - 1, :]), ALU.mult).then_inc(gate_read, 1)
                    dve.wait_ge(gate_read, it * GATE_USES)
                    need(dve, stored, it * 16 - 16)
                    nc.vector.tensor_tensor(out_sb[:, :, :], ffn_sb[:, :, :], x2[:, :, :], ALU.add).then_inc(out_ready, 1)

            def v_read(it):
                if isinstance(it, int) and it == 0:
                    return misc_at(-1, (0, "v", 0)) + 1
                if isinstance(it, int) and it == 7:
                    return misc_at(8 - 1, misc_uses(7)[0]) - tail(1)
                kind = 1 if not isinstance(it, int) else it
                return misc_at(it, misc_uses(kind)[0]) - tail(kind)

            def tail(kind):
                uses = misc_uses(1)
                return len(uses) - 1 - uses.index((2, "v", 0))

            walk(dve, run)

        @block.tensor
        def _(pe):
            pe.wait_ge(const_done, 2)
            pe.wait_ge(ct_step, 2)
            nc.tensor.transpose(pv_bank[:, 0:B], cond_s[:, :], ident[0:B, 0:B]).then_inc(cond_mm, 1)
            pe.wait_ge(ct_step, 4)
            for i, j in enumerate((0, 1, 3, 4)):
                last = nc.tensor.matmul(up_bank[:, B * i:B * (i + 1)], wmod_sb[:, C * j:C * (j + 1)], cond_T[:, :],
                                        start=True, stop=True)
            last.then_inc(cond_mm, 1)
            for banks, j in ((s1_bank, 2), (s2_bank, 5)):
                for b in range(B):
                    last = nc.tensor.matmul(banks[b // 4][:, C * (b % 4):C * (b % 4 + 1)], cond_rep[:, b, :],
                                            wmod_sb[:, C * j:C * (j + 1)], start=True, stop=True)
            last.then_inc(cond_mm, 1)
            pe.wait_ge(w_in, 16 * N_WEIGHTS)

            def take_misc(it, task):
                need(pe, misc_read, misc_at(it, task))

            def transposes(dst, src, idn):
                for t in range(TT):
                    last = nc.tensor.transpose(dst[:, P * t:P * (t + 1)], src(t), idn[:, :])
                return last

            def run(it, s, name, a):
                if name == "xt":
                    pe.wait_ge(x_norm, it + 2)
                    take_misc(it, (s, "xt", 0))
                    transposes(misc, lambda t: x_n[:, t, :], ident).then_inc(misc_written, 1)
                if name in ("q", "k"):
                    take_misc(it, (s, name, 0))
                    nc.tensor.matmul(misc[:, :], (wq if name == "q" else wk)[:, :], h1T[:, :],
                                     start=True, stop=True).then_inc(misc_written, 1)
                if name == "v":
                    take_misc(it, (s, "v", 0))
                    for t in range(TT):
                        last = nc.tensor.matmul(misc_tok[:, t, :], h1T[:, P * t:P * (t + 1)], wv[:, :],
                                                start=True, stop=True)
                    last.then_inc(misc_written, 1)
                if name == "s1":
                    u = U1 * s + a
                    h0, nh, qt = S1_UNITS[a]
                    if a == 0:
                        if isinstance(it, int) and it == 0 and s == 0:
                            pe.wait_ge(gates_read, 2)
                            pe.wait_ge(const_step, 4 + PARTS)
                        pe.wait_ge(stacked[s], it * (16 * Q_DMAS) + 16 * Q_DMAS)
                    need(pe, s1_reduced, it * (G * U1) + (u - 1))
                    w = P * (qt + 1)
                    dst = s1_bank[u % 2]
                    for i in range(nh):
                        h = GH * s + h0 + i
                        nc.tensor.matmul(dst[:, w * i:w * (i + 1)], q_stack[0:KROWS, h, P * qt:P * (qt + 1)],
                                         k_stack[0:KROWS, h, 0:w], start=True, stop=False)
                        last = nc.tensor.matmul(dst[:, w * (i + 1) - P:w * (i + 1)], ident_bf[:, :], causal[:, :],
                                                start=False, stop=True)
                    last.then_inc(s1_written, 1)
                if name == "s2":
                    u = U2 * (s - 1) + a
                    g = (s - 1) % G
                    if a == 0:
                        pe.wait_ge(max_landed, it * (16 * G) + 16 * s)
                    need(pe, exp_done, it * (G * U2) + (u - 1))
                    dst, at = s2_bank[u % 2], 0
                    for h, j in S2_UNITS[a]:
                        w = T - P * j
                        hh = GH * g + h
                        last = nc.tensor.matmul(dst[:, at:at + w], k_stack[0:MROWS, hh, P * j:P * (j + 1)],
                                                q_stack[0:MROWS, hh, P * j:T], start=True, stop=True)
                        at += w
                    last.then_inc(s2_written, 1)
                if name == "pv":
                    g = (s - 1) % G
                    j, units = PV_ORDER[a]
                    pe.wait_ge(probs_ready, it * (G * U2) + (U2 * (s - 1) + units))
                    if a == 0:
                        need(pe, u_ready, it * G + (s - 1))
                        pe.wait_ge(v_ready, it + (1 if s > 0 else 0))
                    for h in range(GH):
                        last = nc.tensor.matmul(pv_bank[VC * h:VC * (h + 1), P * j:T], v_aug[:, j, GH * g + h, :],
                                                probs[g % 2][:, h, P_AT[j]:P_AT[j] + T - P * j],
                                                start=(a == 0), stop=(a == len(PV_ORDER) - 1))
                    if a == len(PV_ORDER) - 1:
                        last.then_inc(pv_done, 1)
                if name == "max":
                    need_all(pe, (const_done, 2), (max_split, it * G + (s + 1)), (misc_read, misc_at(it, (s, "max", 0))))
                    nc.tensor.transpose(misc_bf[0:PARTS * GH * TT, 0:P],
                                        max_parts[:, :, :].rearrange("p a b -> p (a b)"),
                                        ident_bf[:, :]).then_inc(misc_written, 1)
                if name == "o":
                    pe.wait_ge(u_ready, it * G + (s - 1))
                    take_misc(it, (s, "o", 0))
                    transposes(misc, lambda t: u_sb[:, P * t:P * (t + 1)], ident).then_inc(misc_written, 1)
                if name == "ot":
                    take_misc(it, (s, "ot", 0))
                    transposes(misc, lambda t: o_tok[:, t, :], ident).then_inc(misc_written, 1)
                if name == "y":
                    take_misc(it, (s, "y", 0))
                    for t in range(TT):
                        last = nc.tensor.matmul(misc_tok[:, t, :], oT[:, P * t:P * (t + 1)], wo[:, :],
                                                start=True, stop=True)
                    last.then_inc(misc_written, 1)
                if name == "x2t":
                    pe.wait_ge(x2_norm, it)
                    take_misc(it, (s, "x2t", 0))
                    transposes(misc, lambda t: x2_n[:, t, :], ident).then_inc(misc_written, 1)
                if name == "lg":
                    take_misc(it, (s, "lg", 0))
                    for t in range(TT):
                        last = nc.tensor.matmul(misc_tok[:, t, :], h2T[:, P * t:P * (t + 1)], w_router[:, :],
                                                start=True, stop=True)
                    last.then_inc(misc_written, 1)
                if name == "ct":
                    pe.wait_ge(coef_split, it)
                    take_misc(it, (s, "ct", 0))
                    transposes(misc_bf, lambda t: coef_parts[:, t, :], ident_bf).then_inc(misc_written, 1)
                if name == "g":
                    need(pe, gate_read, it * GATE_USES + (a - GATE_USES))
                    nc.tensor.matmul(gate_bank[:, :], wg[:, P * a:P * (a + 1)], h2T[:, :], start=True,
                                     stop=True).then_inc(gate_written, 1)
                if name == "u":
                    need(pe, up_read, it * MB + (a - MB))
                    nc.tensor.matmul(up_bank[:, :], wu[:, P * a:P * (a + 1)], h2T[:, :], start=True,
                                     stop=True).then_inc(up_written, 1)
                if name == "c":
                    take_misc(it, (s, "c", a))
                    nc.tensor.matmul(misc[:, :], pick[:, a, :, :].rearrange("p a b -> p (a b)"), coef_T[:, :],
                                     start=True, stop=True).then_inc(misc_written, 1)
                if name == "down":
                    pe.wait_ge(up_read, it * MB)
                    pe.wait_ge(misc_read, misc_at(it, (3, "c", FB - 1)) + 1)
                    pe.wait_ge(gate_read, it * GATE_USES - 1)
                    for t in range(TT):
                        for m in range(MB):
                            last = nc.tensor.matmul(gate_bank[:, P * t:P * (t + 1)], hidden[:, m, P * t:P * (t + 1)],
                                                    wd[:, m, :], start=(m == 0), stop=(m == MB - 1))
                    last.then_inc(down_written, 1)

            walk(pe, run)


_INS = ["L0_attn_x", "L0_attn_Wq", "L0_attn_bq", "L0_attn_Wk", "L0_attn_bk", "L0_attn_Wv", "L0_attn_bv",
        "L0_attn_Wo", "L0_attn_bo", "L0_attn_gamma", "L0_attn_beta", "L0_ffn_router", "L0_ffn_experts_gate",
        "L0_ffn_experts_up", "L0_ffn_experts_down", "L0_ffn_shared_gate", "L0_ffn_shared_up",
        "L0_ffn_shared_down", "L0_c", "L0_wmod"]


def kernel(**inputs):
    import numpy as np
    import concourse.bacc as bacc
    from concourse.bass_utils import run_bass_kernel_spmd

    nc = bacc.Bacc("TRN2", target_bir_lowering=False, num_devices=1)
    arrays, args = {}, []
    for name in _INS:
        a = np.ascontiguousarray(inputs[name])
        arrays[f"in_{name}"] = a
        args.append(nc.dram_tensor(f"in_{name}", a.shape, mybir.dt.from_np(a.dtype), kind="ExternalInput").ap())
    args.append(nc.dram_tensor("out_x", (B, T, C), F32, kind="ExternalOutput").ap())
    block_kernel(nc, *args)
    r = run_bass_kernel_spmd(nc, [arrays], core_ids=[0])
    return r.results[0]["out_x"]
```

```python
from contextlib import ExitStack

import numpy as np

import concourse.bass as bass
from concourse import mybir

F32 = mybir.dt.float32
BF16 = mybir.dt.bfloat16
ALU = mybir.AluOpType
ACT = mybir.ActivationFunctionType
AX_X = mybir.AxisListType.X

P = 128
B = 8
T = 512
TT = T // P
C = 128
H = 16
DH = C // H
GH = 4
G = H // GH
NG = B * G
PARTS = 3
KROWS = PARTS * PARTS * DH
MROWS = KROWS + PARTS
SROWS = PARTS * DH
E = 8
DE = 64
FB = E * DE // P
MB = FB + 1
VC = 32
EPS = 1e-5
SCALE = DH ** -0.5
MASKED = -3.0e38

S1_UNITS = ([(h, 1, 3) for h in range(GH)] + [(h, 1, 2) for h in range(GH)]
            + [(0, 2, 1), (2, 2, 1)] + [(0, 4, 0)])
S2_UNITS = ([[(h, 0)] for h in range(GH)] + [[(h, 1), (h, 3)] for h in range(GH)]
            + [[(0, 2), (1, 2)], [(2, 2), (3, 2)]])
U1, U2 = len(S1_UNITS), len(S2_UNITS)
P_AT = {0: 0, 1: 512, 3: 896, 2: 1024}
P_LEN = 1280
PV_ORDER = [(0, 4), (1, 8), (3, 8), (2, 10)]

EXTRA = {
    0: {0: [("xres", "prev"), ("xin", "next")], 4: [("uev", ""), ("xs", "next")], 6: [("o", "")],
        7: [("xn", "next")], 9: [("xt", "next")], 11: [("msplit", "cur"), ("q", "next")],
        12: [("max", "cur")], 14: [("k", "next")]},
    1: {4: [("uev", ""), ("vaug", "cur")], 6: [("o", "")], 8: [("ot", "prev")], 10: [("y", "prev")],
        11: [("msplit", "cur"), ("yn", "prev")], 12: [("max", "cur")], 13: [("v", "next"), ("stack", "next")],
        14: [("x2", "prev")]},
    2: {1: [("x2n", "prev")], 3: [("x2t", "prev")], 4: [("uev", "")], 5: [("lg", "prev"), ("route", "prev")],
        6: [("g0", "prev")], 7: [("u0", "prev"), ("prob", "prev")], 8: [("o", "")], 9: [("g1", "prev"), ("above", "prev")],
        10: [("u1", "prev"), ("rank", "prev")], 11: [("msplit", "cur"), ("g2", "prev")],
        12: [("max", "cur")], 13: [("u2", "prev")], 14: [("ct", "prev")]},
    3: {1: [("c0", "prev")], 2: [("g3", "prev")], 3: [("c1", "prev"), ("u3", "prev")],
        4: [("uev", ""), ("g4", "prev")], 5: [("c2", "prev")], 6: [("u4", "prev")], 7: [("c3", "prev")], 9: [("o", "")],
        11: [("msplit", "cur"), ("down0", "prev")], 12: [("max", "cur"), ("down1", "prev")], 13: [("down2", "prev")],
        14: [("down3", "prev"), ("fin", "prev")]},
}
PV_STEPS = [14, 0, 1, 2]
S2_LAG = 5


def slots(has_prev, has_cur, has_next):
    live = {"prev": has_prev, "cur": has_cur, "next": has_next}
    out = []
    for s in range(G):
        s1 = has_cur
        s2 = has_cur if s > 0 else has_prev
        o = has_prev if s < 2 else has_cur
        for k in range(U2 + S2_LAG):
            if s1 and k == 0:
                out.append((s, "load", 0))
            if s1 and k < U1:
                out.append((s, "s1", k))
            if s2 and k >= S2_LAG:
                out.append((s, "s2", k - S2_LAG))
            if s2 and k == PV_STEPS[0]:
                out.append((s, "pv", 0))
            if o and k in PV_STEPS[1:]:
                out.append((s, "pv", PV_STEPS.index(k)))
            for name, whose in EXTRA[s].get(k, []):
                if (whose == "" and o) or (whose and live[whose]):
                    out.append((s, name, 0) if name[-1] not in "01234" or name == "x2"
                               else (s, name[:-1], int(name[-1])))
    return out


PROLOGUE = [(0, t, 0) for t in ("xin", "xs", "cond", "xn", "xt", "q", "k", "stack", "v", "gates")]
KINDS = {-1: PROLOGUE, 0: slots(False, True, True), 1: slots(True, True, True),
         B - 1: slots(True, True, False), B: slots(True, False, False)}
LOOP = (1, B - 1)

MISC_TASKS = ("o", "ot", "y", "x2t", "lg", "ct", "c", "xt", "q", "k", "v", "max")


def misc_uses(kind):
    return [x for x in KINDS[kind] if x[1] in MISC_TASKS]


def misc_at(it, task):
    before = len(misc_uses(-1))
    if isinstance(it, int) and it <= 0:
        return (before if it == 0 else 0) + misc_uses(it).index(task)
    before += len(misc_uses(0))
    each = len(misc_uses(1))
    if isinstance(it, int) and it >= LOOP[1]:
        before += (LOOP[1] - 1) * each + (len(misc_uses(B - 1)) if it == B else 0)
        return before + misc_uses(it).index(task)
    return it * each + (before - each + misc_uses(1).index(task))


def need(eng, sem, value):
    if not isinstance(value, int) or value > 0:
        eng.wait_ge(sem, value)


def need_all(eng, const, *waits):
    waits = [(m, v if isinstance(v, int) else eng.to_reg(v)) for m, v in waits]
    eng.wait_ge(*const)
    for m, v in waits:
        need(eng, m, v)


def walk(eng, run):
    for it in (-1, 0):
        for s, name, a in KINDS[it]:
            run(it, s, name, a)
    with eng.Fori(*LOOP) as it:
        for s, name, a in KINDS[1]:
            run(it, s, name, a)
    for it in (B - 1, B):
        for s, name, a in KINDS[it]:
            run(it, s, name, a)


def block_kernel(nc, x, Wq, bq, Wk, bk, Wv, bv, Wo, bo, gamma, beta, router, w_gate, w_up, w_down,
                 sh_gate, sh_up, sh_down, cond, wmod, out):
    q_scr = nc.dram_tensor("q_scr", [P, PARTS, T], BF16, kind="Internal").ap()
    k_scr = [nc.dram_tensor(f"k_scr{r}", [P, PARTS, T], BF16, kind="Internal").ap()
             for r in range(PARTS)]

    with ExitStack() as ctx:
        def sb(name, shape, dt=F32):
            return ctx.enter_context(nc.sbuf_tensor(name, shape, dt))

        def bank(name):
            return ctx.enter_context(nc.psum_tensor(name, [P, 512], F32))

        def sem(name):
            return ctx.enter_context(nc.semaphore(name))

        s1_bank = [bank("s1_bank0"), bank("s1_bank1")]
        s2_bank = [bank("s2_bank0"), bank("s2_bank1")]
        pv_bank, misc, gate_bank, up_bank = (bank(x) for x in ("pv_bank", "misc", "gate_bank", "up_bank"))
        misc_tok = misc[:, :].rearrange("p (t c) -> p t c", t=TT)
        misc_bf = misc[:, :].bitcast(BF16)

        wq, wk, wv, wo = (sb(x, [P, C]) for x in ("wq", "wk", "wv", "wo"))
        wg, wu = sb("wg", [P, MB * P]), sb("wu", [P, MB * P])
        wd = sb("wd", [P, MB, C])
        w_router = sb("w_router", [P, P])
        bq_col, bk_col = sb("bq_col", [P, 1]), sb("bk_col", [P, 1])
        bv_row, bo_row, gamma_row, beta_row = (sb(x, [P, C]) for x in ("bv_row", "bo_row", "gamma_row", "beta_row"))
        wmod_sb = sb("wmod_sb", [P, 6 * C])
        cond_sb, cond_t, cond_s = (sb(x, [B, P]) for x in ("cond_sb", "cond_t", "cond_s"))
        cond_T = sb("cond_T", [P, B])
        cond_rep = sb("cond_rep", [P, B, P])
        mod_cols = sb("mod_cols", [P, 4, B])
        gate_a, gate_b = sb("gate_a", [P, B, C]), sb("gate_b", [P, B, C])
        gate_sign, gate_abs = sb("gate_sign", [P, B, C]), sb("gate_abs", [P, B, C])
        gamma_a, beta_a = sb("gamma_a", [P, B, C]), sb("beta_a", [P, B, C])
        ident, ident_bf = sb("ident", [P, P]), sb("ident_bf", [P, P], BF16)
        causal = sb("causal", [P, P], BF16)
        pick = sb("pick", [P, FB, 2, DE], BF16)
        earlier = sb("earlier", [P, E, E])
        neg_half = sb("neg_half", [P, TT])
        x_in, x_n = sb("x_in", [P, TT, C]), sb("x_n", [P, TT, C])
        h1T = sb("h1T", [P, T])
        q_parts, k_parts = sb("q_parts", [P, PARTS, T], BF16), sb("k_parts", [P, PARTS, T], BF16)
        q_rest, k_rest = sb("q_rest", [P, T]), sb("k_rest", [P, T])
        v_tok = sb("v_tok", [P, TT, C])
        q_stack, k_stack = sb("q_stack", [P, H, T], BF16), sb("k_stack", [P, H, T], BF16)
        v_aug = sb("v_aug", [P, TT, H, VC])
        row_max = [sb(f"row_max{i}", [P, GH, TT]) for i in range(2)]
        max_parts = sb("max_parts", [P, PARTS, GH * TT], BF16)
        max_rest = sb("max_rest", [P, GH * TT])
        max_rows = sb("max_rows", [PARTS * GH * TT, P], BF16)
        probs = [sb(f"probs{i}", [P, GH, P_LEN]) for i in range(2)]
        u_sb = sb("u_sb", [P, T])
        denom = sb("denom", [P, TT * GH])
        o_tok = sb("o_tok", [P, TT, C])
        oT = sb("oT", [P, T])
        x_res, y_sb, x2, x2_n = (sb(x, [P, TT, C]) for x in ("x_res", "y_sb", "x2", "x2_n"))
        h2T = sb("h2T", [P, T])
        stats = {k: sb(f"stats_{k}", [P, TT, 6]) for k in ("x", "y", "x2")}
        mean_var = {k: sb(f"mean_var_{k}", [P, TT, 2]) for k in ("x", "y", "x2")}
        var_eps = {k: sb(f"var_eps_{k}", [P, TT]) for k in ("x", "y", "x2")}
        rstd = {k: sb(f"rstd_{k}", [P, TT]) for k in ("x", "y", "x2")}
        lmax, esum, erec = (sb(x, [P, TT]) for x in ("lmax", "esum", "erec"))
        logit, expo, prob, rank, coef, coef_rest = (
            sb(x, [P, TT, E]) for x in ("logit", "expo", "prob", "rank", "coef", "coef_rest"))
        above, equal = sb("above", [P, TT, E, E]), sb("equal", [P, TT, E, E])
        coef_parts = sb("coef_parts", [P, TT, P], BF16)
        coef_T = sb("coef_T", [P, T], BF16)
        tanh_sb, silu_sb = sb("tanh_sb", [P, T]), sb("silu_sb", [P, T])
        hidden = sb("hidden", [P, MB, T])
        coef_sb = sb("coef_sb", [P, T])
        ffn_sb, out_sb = sb("ffn_sb", [P, TT, C]), sb("out_sb", [P, TT, C])

        qkv_in = sem("qkv_in")
        rows_in = sem("rows_in")
        ffn_in = sem("ffn_in")
        cond_in = sem("cond_in")
        const_step = sem("const_step")
        const_done = sem("const_done")
        minus_ones = sem("minus_ones")
        ct_step = sem("ct_step")
        cond_mm = sem("cond_mm")
        gates_read = sem("gates_read")
        vec_setup = sem("vec_setup")
        x_in_ready, x_stats, x_mv = sem("x_in_ready"), sem("x_stats"), sem("x_mv")
        x_ve, x_rstd, x_norm = sem("x_ve"), sem("x_rstd"), sem("x_norm")
        q_first, k_first = sem("q_first"), sem("k_first")
        q_second, k_second, q_split, k_split = (sem(x) for x in ("q_second", "k_second", "q_split", "k_split"))
        scr_written = sem("scr_written")
        misc_written, misc_read = sem("misc_written"), sem("misc_read")
        stacked = [sem(f"stacked{g}") for g in range(G)]
        s1_written, s1_reduced = sem("s1_written"), sem("s1_reduced")
        s2_written, exp_done, probs_ready = sem("s2_written"), sem("exp_done"), sem("probs_ready")
        max_step, max_landed = sem("max_step"), sem("max_landed")
        pv_done, u_ready, denom_ready, v_ready = (sem(x) for x in ("pv_done", "u_ready", "denom_ready", "v_ready"))
        xres_in, xres_ready = sem("xres_in"), sem("xres_ready")
        y_stats, y_mv, y_ve, y_rstd = (sem(x) for x in ("y_stats", "y_mv", "y_ve", "y_rstd"))
        x2_stats, x2_mv, x2_ve, x2_rstd, x2_norm = (
            sem(x) for x in ("x2_stats", "x2_mv", "x2_ve", "x2_rstd", "x2_norm"))
        y_norm, y_scaled, x2_ready = sem("y_norm"), sem("y_scaled"), sem("x2_ready")
        lmax_ready, logit_ready, expo_ready = sem("lmax_ready"), sem("logit_ready"), sem("expo_ready")
        route_step, coef_ready, coef_step, coef_split = (
            sem(x) for x in ("route_step", "coef_ready", "coef_step", "coef_split"))
        weighted = sem("weighted")
        gate_written, tanh_ready, gate_read = sem("gate_written"), sem("tanh_ready"), sem("gate_read")
        up_written, up_read = sem("up_written"), sem("up_read")
        down_written, ffn_gated, out_ready, stored = (
            sem(x) for x in ("down_written", "ffn_gated", "out_ready", "stored"))
        block = ctx.enter_context(nc.Block())

        QKV_DMAS, ROW_DMAS, FFN_DMAS = 5, 4, 11
        Q_DMAS = 2 * PARTS
        SCR_DMAS = 1 + 1 + 2 * (PARTS - 1)
        GATE_USES = MB + 1
        ROUTE_STEPS = 8

        def tok(dram, b):
            return dram[b].rearrange("(t p) c -> p t c", p=P)

        def over_tiles(row):
            return row.unsqueeze(1).to_broadcast([P, TT, C])

        @block.sync
        def _(sp):
            sp.dma_start(cond_sb[:, :], cond).then_inc(cond_in, 16)
            sp.dma_start(wmod_sb[:, :], wmod).then_inc(cond_in, 16)
            sp.dma_start(x_in[:, :, :], tok(x, 0)).then_inc(x_in_ready, 16)
            for dst, src in ((wq, Wq), (wk, Wk), (wv, Wv)):
                sp.dma_start(dst[:, :], src).then_inc(qkv_in, 16)
            sp.dma_start(bq_col[:, :], bq.unsqueeze(1)).then_inc(qkv_in, 16)
            sp.dma_start(bk_col[:, :], bk.unsqueeze(1)).then_inc(qkv_in, 16)

            def load_stacks(it, g):
                need(sp, s2_written, it * (G * U2) + U2 * (g + 1 - G))
                need(sp, scr_written, it * (16 * SCR_DMAS) + 16 * SCR_DMAS)
                heads = slice(GH * g, GH * g + GH)
                for r in range(PARTS):
                    rows = slice(SROWS * r, SROWS * (r + 1))
                    for stack, scr in ((q_stack, q_scr), (k_stack, k_scr[r])):
                        src = scr.rearrange("(h d) s t -> (d s) h t", d=DH)
                        sp.dma_start(stack[rows, heads, :], src[:, heads, :]).then_inc(stacked[g], 16)

            def run(it, s, name, a):
                if name == "xres":
                    need(sp, x2_ready, it - 1)
                    sp.dma_start(x_res[:, :, :], tok(x, it - 1)).then_inc(xres_in, 16)
                if name == "stack":
                    sp.wait_ge(const_done, 1)
                    for g in range(G):
                        need(sp, stacked[g], it * (16 * Q_DMAS) + 16 * Q_DMAS)
                    sp.wait_ge(q_split, it + 2)
                    sp.dma_start(q_scr, q_parts[:, :, :]).then_inc(scr_written, 16)
                    sp.wait_ge(k_split, it + 2)
                    sp.dma_start(k_scr[0], k_parts[:, :, :]).then_inc(scr_written, 16)
                    for r in range(1, PARTS):
                        sp.dma_start(k_scr[r][:, 0:PARTS - r, :], k_parts[:, r:PARTS, :]).then_inc(scr_written, 16)
                        sp.dma_start(k_scr[r][:, PARTS - r:PARTS, :], k_parts[:, 0:r, :]).then_inc(scr_written, 16)
                    if isinstance(it, int) and it < 0:
                        sp.wait_ge(minus_ones, 1)
                        load_stacks(0, 0)
                        load_stacks(0, 1)
                if name == "load" and s < 2:
                    load_stacks(it, s + 2)
                if name == "load" and s >= 2 and has_next(it):
                    load_stacks(it + 1, s - 2)
                if name == "fin":
                    sp.wait_ge(out_ready, it)
                    sp.dma_start(tok(out, it - 1), out_sb[:, :, :]).then_inc(stored, 16)

            def has_next(it):
                return not isinstance(it, int) or it < B - 1

            walk(sp, run)
            sp.wait_ge(stored, 16 * B)

        @block.gpsimd
        def _(pool):
            nc.gpsimd.memset(ident[:, :], 0.0)
            nc.gpsimd.memset(neg_half[:, :], -0.5)
            nc.gpsimd.memset(ident_bf[:, :], 0.0)
            nc.gpsimd.memset(w_router[:, :], 0.0)
            nc.gpsimd.memset(causal[:, :], 0.0).then_inc(const_step, 1)
            pool.wait_ge(const_step, 1)
            for m in (ident, ident_bf):
                last = nc.gpsimd.affine_select(out=m[:, :], in_=m[:, :], compare_op=ALU.not_equal, fill=1.0,
                                               base=0, pattern=[[-1, P]], channel_multiplier=1)
            last = nc.gpsimd.affine_select(out=causal[:, :], in_=causal[:, :], compare_op=ALU.is_ge, fill=MASKED,
                                           base=0, pattern=[[-1, P]], channel_multiplier=1)
            last.then_inc(const_done, 1)

            def late_constants():
                nc.gpsimd.memset(pick[:, :, :, :], 0.0)
                nc.gpsimd.memset(earlier[:, :, :], 1.0)
                nc.gpsimd.memset(coef_parts[:, :, :], 0.0)
                nc.gpsimd.memset(v_aug[:, :, :, :], 0.0).then_inc(const_step, 1)
                pool.wait_ge(const_step, 2)
                nc.gpsimd.memset(v_aug[:, :, :, DH:DH + 1], 1.0)
                nc.gpsimd.affine_select(out=earlier[:, :, :], in_=earlier[:, :, :], compare_op=ALU.is_ge, fill=0.0,
                                        base=-1, pattern=[[1, E], [-1, E]], channel_multiplier=0).then_inc(const_step, 1)
                for part in range(PARTS):
                    pool.wait_ge(const_step, 3 + part)
                    nc.gpsimd.affine_select(out=pick[:, :, :, :], in_=pick[:, :, :, :], compare_op=ALU.not_equal,
                                            fill=1.0, base=-part * E, pattern=[[-2, FB], [-1, 2], [0, DE]],
                                            channel_multiplier=1).then_inc(const_step, 1)
                pool.wait_ge(const_step, 3 + PARTS)

            def inv_std(key, mv_sem, ve_sem, rstd_sem, b1):
                need_all(pool, (const_done, 1), (mv_sem, b1))
                nc.gpsimd.tensor_scalar(var_eps[key][:, :], mean_var[key][:, :, 1], EPS, None, ALU.add).then_inc(ve_sem, 1)
                pool.wait_ge(ve_sem, b1)
                nc.gpsimd.tensor_tensor(rstd[key][:, :], var_eps[key][:, :], neg_half[:, :], ALU.pow).then_inc(rstd_sem, 1)

            def split_rest(it, name, parts, rest, second, done):
                need_all(pool, (const_done, 1), (misc_read, misc_at(it, name) + 1), (scr_written, it * (16 * SCR_DMAS) + 16 * SCR_DMAS))
                nc.gpsimd.tensor_scalar(parts[:, 1, :], rest[:, :], 1.0, None, ALU.mult).then_inc(second, 1)
                pool.wait_ge(second, it + 2)
                nc.gpsimd.tensor_tensor(parts[:, 2, :], rest[:, :], parts[:, 1, :], ALU.subtract).then_inc(done, 1)

            def run(it, s, name, a):
                if name == "xs":
                    inv_std("x", x_mv, x_ve, x_rstd, it + 2)
                if name == "xn":
                    need_all(pool, (const_done, 1), (x_rstd, it + 2))
                    for t in range(TT):
                        last = nc.gpsimd.tensor_scalar(x_n[:, t, :], x_in[:, t, :], mean_var["x"][:, t, 0:1],
                                                       rstd["x"][:, t:t + 1], ALU.subtract, ALU.mult)
                    last.then_inc(x_norm, 1)
                if name == "gates":
                    late_constants()
                if name == "vaug":
                    need(pool, pv_done, it * G)
                    pool.wait_ge(misc_read, misc_at(it, misc_uses(it if isinstance(it, int) else 1)[0]))
                    pool.wait_ge(rows_in, 16 * ROW_DMAS)
                    nc.gpsimd.tensor_tensor(
                        v_aug[:, :, :, 0:DH], v_tok[:, :, :].rearrange("p t (h d) -> p t h d", h=H),
                        bv_row[:, :].rearrange("p (h d) -> p h d", h=H).unsqueeze(1).to_broadcast([P, TT, H, DH]),
                        ALU.add).then_inc(v_ready, 1)
                if name == "yn":
                    pool.wait_ge(y_norm, it)
                    nc.gpsimd.tensor_tensor(y_sb[:, :, :], y_sb[:, :, :], over_tiles(gamma_a[:, it - 1, :]),
                                            ALU.mult).then_inc(y_scaled, 1)
                if name == "c":
                    pool.wait_ge(misc_read, misc_at(it, (s, "c", a)) + 1)
                    pool.wait_ge(up_read, it * MB + (a + 1 - MB))
                    nc.gpsimd.tensor_tensor(hidden[:, a, :], hidden[:, a, :], coef_sb[:, :], ALU.mult).then_inc(weighted, 1)
                if name == "fin":
                    pool.wait_ge(gate_read, it * GATE_USES)
                    need(pool, stored, it * 16 - 16)
                    nc.gpsimd.tensor_tensor(out_sb[:, :, :], ffn_sb[:, :, :], x2[:, :, :], ALU.add).then_inc(out_ready, 1)
                if name == "q":
                    split_rest(it, (s, "q", 0), q_parts, q_rest, q_second, q_split)
                if name == "k":
                    split_rest(it, (s, "k", 0), k_parts, k_rest, k_second, k_split)
                if name == "s2":
                    ng = (s - 1) % G
                    pr = probs[ng % 2]
                    need_all(pool, (const_done, 1), (exp_done, it * (G * U2) + U2 * (s - 1) + a + 1))
                    h, j = S2_UNITS[a][0]
                    if a < 4:
                        view, pat = pr[:, h, P_AT[0]:P_AT[0] + P], [[1, P]]
                    elif a < 8:
                        at = P_AT[1]
                        step = P_AT[3] - P_AT[1]
                        view = pr[:, h, at:at + 2 * step].rearrange("p (a b) -> p a b", a=2)[:, :, 0:P]
                        pat = [[0, 2], [1, P]]
                    else:
                        view, pat = pr[:, h:h + 2, P_AT[2]:P_AT[2] + P], [[0, 2], [1, P]]
                    nc.gpsimd.affine_select(out=view, in_=view, compare_op=ALU.is_ge, fill=0.0, base=0,
                                            pattern=pat, channel_multiplier=-1).then_inc(probs_ready, 1)
                if name == "y":
                    inv_std("y", y_mv, y_ve, y_rstd, it)
                if name == "x2":
                    inv_std("x2", x2_mv, x2_ve, x2_rstd, it)
                if name == "ot":
                    pool.wait_ge(xres_in, it * 16)
                    pool.wait_ge(vec_setup, 1)
                    nc.gpsimd.tensor_tensor(x_res[:, :, :], x_res[:, :, :], over_tiles(beta_a[:, it - 1, :]),
                                            ALU.add).then_inc(xres_ready, 1)
                if name == "rank":
                    c = coef[:, :, :]
                    cp = [coef_parts[:, :, E * k:E * k + E] for k in range(PARTS)]
                    need_all(pool, (const_done, 1), (coef_ready, it))
                    nc.gpsimd.tensor_scalar(cp[0], c, 1.0, None, ALU.mult).then_inc(coef_step, 1)
                    pool.wait_ge(coef_step, it * 3 - 2)
                    nc.gpsimd.tensor_tensor(coef_rest[:, :, :], c, cp[0], ALU.subtract).then_inc(coef_step, 1)
                    need_all(pool, (const_done, 1), (coef_step, it * 3 - 1))
                    nc.gpsimd.tensor_scalar(cp[1], coef_rest[:, :, :], 1.0, None, ALU.mult).then_inc(coef_step, 1)
                    pool.wait_ge(coef_step, it * 3)
                    nc.gpsimd.tensor_tensor(cp[2], coef_rest[:, :, :], cp[1], ALU.subtract).then_inc(coef_split, 1)

            walk(pool, run)

        @block.scalar
        def _(act):
            act.wait_ge(cond_in, 32)
            nc.scalar.activation(cond_t[:, :], cond_sb[:, :], ACT.Tanh, scale=0.5).then_inc(ct_step, 1)
            for dst, src in ((bv_row, bv), (gamma_row, gamma), (beta_row, beta), (bo_row, bo)):
                act.dma_start(dst[:, :], src.unsqueeze(0).to_broadcast([P, C])).then_inc(rows_in, 16)
            act.dma_start(wo[:, :], Wo).then_inc(ffn_in, 16)
            act.wait_ge(const_done, 1)
            act.dma_start(w_router[:, 0:E], router).then_inc(ffn_in, 16)
            for dst, experts, shared in ((wg, w_gate, sh_gate), (wu, w_up, sh_up)):
                act.dma_start(dst[:, 0:FB * P].rearrange("p (e d) -> p e d", e=E),
                              experts.rearrange("e h d -> h e d")).then_inc(ffn_in, 16)
                act.dma_start(dst[:, FB * P:MB * P], shared).then_inc(ffn_in, 16)
            for m in range(FB):
                act.dma_start(wd[:, m, :], w_down[2 * m:2 * m + 2].rearrange("e d h -> (e d) h")).then_inc(ffn_in, 16)
            act.dma_start(wd[:, FB, :], sh_down).then_inc(ffn_in, 16)
            act.wait_ge(ct_step, 6)
            act.wait_ge(qkv_in, 16 * QKV_DMAS)

            def part_first(it, name, col, parts, first):
                act.wait_ge(misc_written, misc_at(it, name) + 1)
                need(act, scr_written, it * (16 * SCR_DMAS) + 16 * SCR_DMAS)
                nc.scalar.activation(parts[:, 0, :], misc[:, :], ACT.Identity, bias=col[:, 0:1]).then_inc(first, 1)

            def run(it, s, name, a):
                if name == "xin" and not (isinstance(it, int) and it == -1):
                    need(act, x_norm, it + 1)
                    act.dma_start(x_in[:, :, :], tok(x, it + 1)).then_inc(x_in_ready, 16)
                if name == "xt":
                    act.wait_ge(misc_written, misc_at(it, (s, "xt", 0)) + 1)
                    nc.scalar.activation(h1T[:, :], misc[:, :], ACT.Identity, scale=mod_cols[:, 1, it + 1].unsqueeze(1),
                                         bias=mod_cols[:, 0, it + 1].unsqueeze(1)).then_inc(misc_read, 1)
                if name == "q":
                    part_first(it, (s, "q", 0), bq_col, q_parts, q_first)
                if name == "k":
                    part_first(it, (s, "k", 0), bk_col, k_parts, k_first)
                if name == "v":
                    act.wait_ge(misc_written, misc_at(it, (s, "v", 0)) + 1)
                    need(act, v_ready, it + 1)
                    nc.scalar.activation(v_tok[:, :, :], misc_tok, ACT.Copy).then_inc(misc_read, 1)
                if name == "s2":
                    pr = probs[(s - 1) % G % 2]
                    u = U2 * (s - 1) + a
                    act.wait_ge(s2_written, it * (G * U2) + (u + 1))
                    h, j = S2_UNITS[a][0]
                    src = s2_bank[u % 2][:, :]
                    if a < 8:
                        at = P_AT[j]
                        dst = pr[:, h, at:at + 512]
                    else:
                        dst = pr[:, h:h + 2, P_AT[2]:P_AT[2] + 256]
                        src = src.rearrange("p (a b) -> p a b", a=2)
                    nc.scalar.activation(dst, src, ACT.Exp, scale=SCALE).then_inc(exp_done, 1)
                if name == "uev":
                    act.wait_ge(pv_done, it * G + (s - 1))
                    if not (isinstance(it, int) and (it, s) == (0, 2)):
                        if s > 0:
                            act.wait_ge(misc_written, misc_at(it, (s - 1, "o", 0)) + 1)
                        else:
                            act.wait_ge(misc_written, misc_at(it, misc_uses(it if isinstance(it, int) else 1)[0]))
                    nc.scalar.activation(u_sb[:, :], pv_bank[:, :], ACT.Copy).then_inc(u_ready, 1)
                if name == "max":
                    k = misc_at(it, (s, "max", 0)) + 1
                    act.wait_ge(misc_written, k)
                    need(act, max_landed, it * (16 * G) + 16 * s)
                    nc.scalar.activation(max_rows[:, :], misc_bf[0:PARTS * GH * TT, 0:P], ACT.Copy).then_inc(misc_read, 1)
                    act.wait_ge(misc_read, k)
                    act.dma_start(q_stack[KROWS:MROWS, GH * s:GH * s + GH, :].rearrange("p h (b t) -> p (h b) t", t=P),
                                  max_rows[:, :]).then_inc(max_landed, 16)
                if name == "ot":
                    act.wait_ge(misc_written, misc_at(it, (s, "ot", 0)) + 1)
                    nc.scalar.activation(oT[:, :], misc[:, :], ACT.Copy).then_inc(misc_read, 1)
                if name == "x2t":
                    act.wait_ge(misc_written, misc_at(it, (s, "x2t", 0)) + 1)
                    nc.scalar.activation(h2T[:, :], misc[:, :], ACT.Identity, scale=mod_cols[:, 3, it - 1].unsqueeze(1),
                                         bias=mod_cols[:, 2, it - 1].unsqueeze(1)).then_inc(misc_read, 1)
                if name == "route":
                    act.wait_ge(logit_ready, it)
                    nc.scalar.activation(expo[:, :, :], logit[:, :, :], ACT.Exp).then_inc(expo_ready, 1)
                if name == "ct":
                    act.wait_ge(misc_written, misc_at(it, (s, "ct", 0)) + 1)
                    nc.scalar.activation(coef_T[:, :], misc_bf[:, 0:T], ACT.Copy).then_inc(misc_read, 1)
                if name == "c":
                    act.wait_ge(misc_written, misc_at(it, (s, "c", a)) + 1)
                    need(act, weighted, it * FB + (a - FB))
                    nc.scalar.activation(coef_sb[:, :], misc[:, :], ACT.Copy).then_inc(misc_read, 1)
                if name == "g":
                    act.wait_ge(gate_written, it * MB + (a + 1 - MB))
                    if a > 0:
                        act.wait_ge(gate_read, it * GATE_USES + (a - GATE_USES))
                    nc.scalar.activation(tanh_sb[:, :], gate_bank[:, :], ACT.Tanh, scale=0.5).then_inc(tanh_ready, 1)

            walk(act, run)

        @block.vector
        def _(dve):
            nc.vector.memset(k_stack[64:MROWS, :, :].rearrange("p h t -> p (h t)").bitcast(F32),
                             float(np.array([0xBF80BF80], np.uint32).view(np.float32)[0])).then_inc(minus_ones, 1)

            def condition():
                dve.wait_ge(ct_step, 1)
                nc.vector.scalar_tensor_tensor(cond_s[:, :], cond_t[:, :], 1.0, cond_sb[:, :], ALU.add,
                                               ALU.mult).then_inc(ct_step, 1)
                dve.wait_ge(cond_mm, 1)
                nc.vector.tensor_scalar(cond_T[:, :], pv_bank[:, 0:B], 0.5, None, ALU.mult).then_inc(ct_step, 1)
                dve.wait_ge(cond_mm, 2)
                nc.vector.tensor_copy(mod_cols[:, 0::2, :], up_bank[:, 0:2 * B].rearrange("p (j b) -> p j b", j=2)).then_inc(ct_step, 1)
                nc.vector.tensor_scalar(mod_cols[:, 1::2, :], up_bank[:, 2 * B:4 * B].rearrange("p (j b) -> p j b", j=2),
                                        1.0, None, ALU.add).then_inc(ct_step, 1)
                dve.wait_ge(ct_step, 5)
                nc.vector.tensor_copy(cond_rep[:, :, :], cond_T[:, :].unsqueeze(2).to_broadcast([P, B, P])).then_inc(ct_step, 1)

            def gates():
                dve.wait_ge(cond_mm, 3)
                for banks, gate in ((s1_bank, gate_a), (s2_bank, gate_b)):
                    for j in range(B // 4):
                        last = nc.vector.tensor_copy(gate[:, 4 * j:4 * j + 4, :],
                                                     banks[j][:, :].rearrange("p (b c) -> p b c", b=4))
                    last.then_inc(gates_read, 1)
                for i, gate in enumerate((gate_a, gate_b)):
                    dve.wait_ge(gates_read, i + 1)
                    dve.wait_ge(ct_step, 6 + 4 * i)
                    nc.vector.tensor_scalar(gate_sign[:, :, :], gate[:, :, :], 0.0, 2.0, ALU.is_ge, ALU.mult).then_inc(ct_step, 1)
                    dve.wait_ge(ct_step, 7 + 4 * i)
                    nc.vector.tensor_scalar(gate_sign[:, :, :], gate_sign[:, :, :], -1.0, None, ALU.add).then_inc(ct_step, 1)
                    dve.wait_ge(ct_step, 8 + 4 * i)
                    nc.vector.tensor_tensor(gate_abs[:, :, :], gate[:, :, :], gate_sign[:, :, :], ALU.mult).then_inc(ct_step, 1)
                    dve.wait_ge(ct_step, 9 + 4 * i)
                    nc.vector.scalar_tensor_tensor(gate[:, :, :], gate_abs[:, :, :], 0.25, gate_sign[:, :, :], ALU.max,
                                                   ALU.mult).then_inc(ct_step, 1)
                dve.wait_ge(rows_in, 16 * ROW_DMAS)
                dve.wait_ge(ct_step, 14)
                nc.vector.tensor_tensor(gamma_a[:, :, :], gate_a[:, :, :],
                                        gamma_row[:, :].unsqueeze(1).to_broadcast([P, B, C]), ALU.mult)
                nc.vector.tensor_tensor(beta_a[:, :, :], gate_a[:, :, :],
                                        beta_row[:, :].unsqueeze(1).to_broadcast([P, B, C]), ALU.mult).then_inc(vec_setup, 1)
                dve.wait_ge(vec_setup, 1)

            def layer_stats(key, src, st_sem, mv_sem, b1):
                for t in range(TT):
                    last = nc.vector.bn_stats(stats[key][:, t, :], src[:, t, :])
                last.then_inc(st_sem, 1)
                need_all(dve, (const_done, 1), (st_sem, b1))
                for t in range(TT):
                    last = nc.vector.bn_aggr(mean_var[key][:, t, :], stats[key][:, t, :])
                last.then_inc(mv_sem, 1)

            def normalise(key, dst, src, rstd_sem, norm_sem, b1):
                dve.wait_ge(rstd_sem, b1)
                for t in range(TT):
                    last = nc.vector.tensor_scalar(dst[:, t, :], src[:, t, :], mean_var[key][:, t, 0:1],
                                                   rstd[key][:, t:t + 1], ALU.subtract, ALU.mult)
                last.then_inc(norm_sem, 1)

            def rest_of(it, name, col, parts, rest, first, split):
                dve.wait_ge(first, it + 2)
                need(dve, split, it + 1)
                nc.vector.scalar_tensor_tensor(rest[:, :], misc[:, :], col[:, 0:1], parts[:, 0, :], ALU.add,
                                               ALU.subtract).then_inc(misc_read, 1)

            def run(it, s, name, a):
                if name == "xs":
                    dve.wait_ge(x_in_ready, it * 16 + 32)
                    layer_stats("x", x_in, x_stats, x_mv, it + 2)
                if name == "cond":
                    condition()
                if name == "gates":
                    dve.wait_ge(qkv_in, 16 * QKV_DMAS)
                    gates()
                if name == "q":
                    rest_of(it, name, bq_col, q_parts, q_rest, q_first, q_split)
                if name == "k":
                    rest_of(it, name, bk_col, k_parts, k_rest, k_first, k_split)
                if name == "s1":
                    u = U1 * s + a
                    h, nh, qt = S1_UNITS[a]
                    dve.wait_ge(s1_written, it * (G * U1) + (u + 1))
                    if a == 0:
                        need(dve, max_step, it * (G * 4) + 4 * (s - 1))
                    w = P * (qt + 1)
                    nc.vector.reduce_max(row_max[s % 2][:, h:h + nh, qt],
                                         s1_bank[u % 2][:, 0:nh * w].rearrange("p (h k) -> p h k", h=nh),
                                         AX_X).then_inc(s1_reduced, 1)
                if name == "msplit":
                    rm = row_max[s % 2][:, :, :].rearrange("p h t -> p (h t)")
                    n4, c4 = it * (G * 4), 4 * s
                    need(dve, max_landed, it * (16 * G) + 16 * s)
                    dve.wait_ge(s1_reduced, it * (G * U1) + U1 * (s + 1))
                    nc.vector.tensor_copy(max_parts[:, 0, :], rm).then_inc(max_step, 1)
                    dve.wait_ge(max_step, n4 + (c4 + 1))
                    nc.vector.tensor_tensor(max_rest[:, :], rm, max_parts[:, 0, :], ALU.subtract).then_inc(max_step, 1)
                    dve.wait_ge(max_step, n4 + (c4 + 2))
                    nc.vector.tensor_copy(max_parts[:, 1, :], max_rest[:, :]).then_inc(max_step, 1)
                    dve.wait_ge(max_step, n4 + (c4 + 3))
                    nc.vector.tensor_tensor(max_parts[:, 2, :], max_rest[:, :], max_parts[:, 1, :],
                                            ALU.subtract).then_inc(max_step, 1)
                if name == "o":
                    g = (s - 2) % G
                    dve.wait_ge(misc_written, misc_at(it, (s, "o", 0)) + 1)
                    if g == 0 and not (isinstance(it, int) and it == 0):
                        dve.wait_ge(misc_written, misc_at(it, (1, "ot", 0)) + 1)
                    view = misc[:, :].rearrange("p (c v) -> p c v", v=VC)
                    nc.vector.reciprocal(denom[:, :].unsqueeze(2), view[:, :, DH:DH + 1]).then_inc(denom_ready, 1)
                    dve.wait_ge(denom_ready, it * G + (s - 1))
                    nc.vector.tensor_tensor(
                        o_tok[:, :, GH * DH * g:GH * DH * (g + 1)].rearrange("p t (h d) -> p t h d", h=GH),
                        misc[:, :].rearrange("p (t h v) -> p t h v", t=TT, h=GH)[:, :, :, 0:DH],
                        denom[:, :].rearrange("p (t h) -> p t h", t=TT).unsqueeze(3).to_broadcast([P, TT, GH, DH]),
                        ALU.mult).then_inc(misc_read, 1)
                if name == "y":
                    k = misc_at(it, (s, "y", 0)) + 1
                    dve.wait_ge(misc_written, k)
                    nc.vector.tensor_tensor(y_sb[:, :, :], misc_tok, over_tiles(bo_row[:, :]), ALU.add).then_inc(misc_read, 1)
                    dve.wait_ge(misc_read, k)
                    layer_stats("y", y_sb, y_stats, y_mv, it)
                if name == "yn":
                    normalise("y", y_sb, y_sb, y_rstd, y_norm, it)
                if name == "x2":
                    dve.wait_ge(y_scaled, it)
                    dve.wait_ge(xres_ready, it)
                    nc.vector.tensor_tensor(x2[:, :, :], y_sb[:, :, :], x_res[:, :, :], ALU.add).then_inc(x2_ready, 1)
                    dve.wait_ge(x2_ready, it)
                    layer_stats("x2", x2, x2_stats, x2_mv, it)
                if name == "x2n":
                    normalise("x2", x2_n, x2, x2_rstd, x2_norm, it)
                if name == "route":
                    dve.wait_ge(misc_written, misc_at(it, (s, "lg", 0)) + 1)
                    lg = misc_tok[:, :, 0:E]
                    nc.vector.reduce_max(lmax[:, :], lg, AX_X).then_inc(lmax_ready, 1)
                    dve.wait_ge(lmax_ready, it)
                    nc.vector.tensor_tensor(logit[:, :, :], lg, lmax[:, :].unsqueeze(2).to_broadcast([P, TT, E]),
                                            ALU.subtract).then_inc(logit_ready, 1)
                    dve.wait_ge(logit_ready, it)
                    nc.vector.tensor_scalar(lmax[:, :], lmax[:, :], 1.0, None, ALU.mult).then_inc(misc_read, 1)
                if name == "prob":
                    r0 = it * ROUTE_STEPS - ROUTE_STEPS
                    dve.wait_ge(expo_ready, it)
                    nc.vector.reduce_sum(esum[:, :], expo[:, :, :], AX_X).then_inc(route_step, 1)
                    dve.wait_ge(route_step, r0 + 1)
                    nc.vector.reciprocal(erec[:, :], esum[:, :]).then_inc(route_step, 1)
                    dve.wait_ge(route_step, r0 + 2)
                    nc.vector.tensor_tensor(prob[:, :, :], expo[:, :, :], erec[:, :].unsqueeze(2).to_broadcast([P, TT, E]),
                                            ALU.mult).then_inc(route_step, 1)
                if name == "above":
                    r0 = it * ROUTE_STEPS - ROUTE_STEPS
                    big = [P, TT, E, E]
                    dve.wait_ge(route_step, r0 + 3)
                    other = prob[:, :, :].unsqueeze(2).to_broadcast(big)
                    own = prob[:, :, :].unsqueeze(3).to_broadcast(big)
                    nc.vector.tensor_tensor(equal[:, :, :, :], other, own, ALU.is_equal).then_inc(route_step, 1)
                    nc.vector.tensor_tensor(above[:, :, :, :], other, own, ALU.is_gt).then_inc(route_step, 1)
                    dve.wait_ge(route_step, r0 + 4)
                    nc.vector.tensor_tensor(equal[:, :, :, :], equal[:, :, :, :],
                                            earlier[:, :, :].unsqueeze(1).to_broadcast(big), ALU.mult).then_inc(route_step, 1)
                if name == "rank":
                    r0 = it * ROUTE_STEPS - ROUTE_STEPS
                    dve.wait_ge(route_step, r0 + 6)
                    nc.vector.tensor_tensor(above[:, :, :, :], above[:, :, :, :], equal[:, :, :, :],
                                            ALU.add).then_inc(route_step, 1)
                    dve.wait_ge(route_step, r0 + 7)
                    nc.vector.reduce_sum(rank[:, :, :], above[:, :, :, :], AX_X).then_inc(route_step, 1)
                    dve.wait_ge(route_step, r0 + 8)
                    nc.vector.scalar_tensor_tensor(coef[:, :, :], rank[:, :, :], 1.5, prob[:, :, :], ALU.is_lt,
                                                   ALU.mult).then_inc(coef_ready, 1)
                if name == "g":
                    dve.wait_ge(tanh_ready, it * MB + (a + 1 - MB))
                    need(dve, up_read, it * MB + (a - MB))
                    nc.vector.scalar_tensor_tensor(silu_sb[:, :], tanh_sb[:, :], 1.0, gate_bank[:, :], ALU.add,
                                                   ALU.mult).then_inc(gate_read, 1)
                if name == "u":
                    dve.wait_ge(up_written, it * MB + (a + 1 - MB))
                    dve.wait_ge(gate_read, it * GATE_USES + (a + 1 - GATE_USES))
                    nc.vector.scalar_tensor_tensor(hidden[:, a, :], silu_sb[:, :], 0.5, up_bank[:, :], ALU.mult,
                                                   ALU.mult).then_inc(up_read, 1)
                if name == "fin":
                    need(dve, out_ready, it - 1)
                    dve.wait_ge(down_written, it)
                    nc.vector.tensor_tensor(ffn_sb[:, :, :], gate_bank[:, :].rearrange("p (t c) -> p t c", t=TT),
                                            over_tiles(gate_b[:, it - 1, :]), ALU.mult).then_inc(gate_read, 1)

            walk(dve, run)

        @block.tensor
        def _(pe):
            def condition():
                pe.wait_ge(const_done, 1)
                pe.wait_ge(ct_step, 2)
                nc.tensor.transpose(pv_bank[:, 0:B], cond_s[:, :], ident[0:B, 0:B]).then_inc(cond_mm, 1)
                pe.wait_ge(ct_step, 3)
                for i, j in enumerate((0, 3, 1, 4)):
                    last = nc.tensor.matmul(up_bank[:, B * i:B * (i + 1)], wmod_sb[:, C * j:C * (j + 1)], cond_T[:, :],
                                            start=True, stop=True)
                last.then_inc(cond_mm, 1)

            def gates():
                pe.wait_ge(ct_step, 6)
                for banks, j in ((s1_bank, 2), (s2_bank, 5)):
                    for b in range(B):
                        last = nc.tensor.matmul(banks[b // 4][:, C * (b % 4):C * (b % 4 + 1)], cond_rep[:, b, :],
                                                wmod_sb[:, C * j:C * (j + 1)], start=True, stop=True)
                last.then_inc(cond_mm, 1)

            def take_misc(it, task):
                need(pe, misc_read, misc_at(it, task))

            def transposes(dst, src, idn):
                for t in range(TT):
                    last = nc.tensor.transpose(dst[:, P * t:P * (t + 1)], src(t), idn[:, :])
                return last

            def run(it, s, name, a):
                if name == "cond":
                    condition()
                if name == "gates":
                    gates()
                if name == "v" and isinstance(it, int) and it == 0:
                    pe.wait_ge(ffn_in, 16 * FFN_DMAS)
                if name == "q" and isinstance(it, int):
                    pe.wait_ge(qkv_in, 16 * QKV_DMAS)
                if name == "xt":
                    pe.wait_ge(x_norm, it + 2)
                    take_misc(it, (s, "xt", 0))
                    transposes(misc, lambda t: x_n[:, t, :], ident).then_inc(misc_written, 1)
                if name in ("q", "k"):
                    take_misc(it, (s, name, 0))
                    nc.tensor.matmul(misc[:, :], (wq if name == "q" else wk)[:, :], h1T[:, :],
                                     start=True, stop=True).then_inc(misc_written, 1)
                if name == "v":
                    take_misc(it, (s, "v", 0))
                    for t in range(TT):
                        last = nc.tensor.matmul(misc_tok[:, t, :], h1T[:, P * t:P * (t + 1)], wv[:, :],
                                                start=True, stop=True)
                    last.then_inc(misc_written, 1)
                if name == "s1":
                    u = U1 * s + a
                    h0, nh, qt = S1_UNITS[a]
                    if a == 0:
                        if isinstance(it, int) and it == 0 and s == 0:
                            pe.wait_ge(gates_read, 2)
                            pe.wait_ge(const_step, 3 + PARTS)
                        pe.wait_ge(stacked[s], it * (16 * Q_DMAS) + 16 * Q_DMAS)
                    need(pe, s1_reduced, it * (G * U1) + (u - 1))
                    w = P * (qt + 1)
                    dst = s1_bank[u % 2]
                    for i in range(nh):
                        h = GH * s + h0 + i
                        nc.tensor.matmul(dst[:, w * i:w * (i + 1)], q_stack[0:KROWS, h, P * qt:P * (qt + 1)],
                                         k_stack[0:KROWS, h, 0:w], start=True, stop=False)
                        last = nc.tensor.matmul(dst[:, w * (i + 1) - P:w * (i + 1)], ident_bf[:, :], causal[:, :],
                                                start=False, stop=True)
                    last.then_inc(s1_written, 1)
                if name == "s2":
                    u = U2 * (s - 1) + a
                    g = (s - 1) % G
                    if a == 0:
                        pe.wait_ge(max_landed, it * (16 * G) + 16 * s)
                    need(pe, exp_done, it * (G * U2) + (u - 1))
                    dst, at = s2_bank[u % 2], 0
                    for h, j in S2_UNITS[a]:
                        w = T - P * j
                        hh = GH * g + h
                        last = nc.tensor.matmul(dst[:, at:at + w], k_stack[0:MROWS, hh, P * j:P * (j + 1)],
                                                q_stack[0:MROWS, hh, P * j:T], start=True, stop=True)
                        at += w
                    last.then_inc(s2_written, 1)
                if name == "pv":
                    n = s - 1 if a == 0 else s - 2
                    g = n % G
                    j, units = PV_ORDER[a]
                    pe.wait_ge(probs_ready, it * (G * U2) + (U2 * n + units))
                    if a == 0:
                        need(pe, u_ready, it * G + (s - 1))
                        pe.wait_ge(v_ready, it + (1 if s > 0 else 0))
                    for h in range(GH):
                        last = nc.tensor.matmul(pv_bank[VC * h:VC * (h + 1), P * j:T], v_aug[:, j, GH * g + h, :],
                                                probs[g % 2][:, h, P_AT[j]:P_AT[j] + T - P * j],
                                                start=(a == 0), stop=(a == len(PV_ORDER) - 1))
                    if a == len(PV_ORDER) - 1:
                        last.then_inc(pv_done, 1)
                if name == "max":
                    need_all(pe, (const_done, 1), (max_step, it * (G * 4) + 4 * (s + 1)), (misc_read, misc_at(it, (s, "max", 0))))
                    nc.tensor.transpose(misc_bf[0:PARTS * GH * TT, 0:P],
                                        max_parts[:, :, :].rearrange("p a b -> p (a b)"),
                                        ident_bf[:, :]).then_inc(misc_written, 1)
                if name == "o":
                    pe.wait_ge(u_ready, it * G + (s - 1))
                    take_misc(it, (s, "o", 0))
                    transposes(misc, lambda t: u_sb[:, P * t:P * (t + 1)], ident).then_inc(misc_written, 1)
                if name == "ot":
                    take_misc(it, (s, "ot", 0))
                    transposes(misc, lambda t: o_tok[:, t, :], ident).then_inc(misc_written, 1)
                if name == "y":
                    take_misc(it, (s, "y", 0))
                    for t in range(TT):
                        last = nc.tensor.matmul(misc_tok[:, t, :], oT[:, P * t:P * (t + 1)], wo[:, :],
                                                start=True, stop=True)
                    last.then_inc(misc_written, 1)
                if name == "x2t":
                    pe.wait_ge(x2_norm, it)
                    take_misc(it, (s, "x2t", 0))
                    transposes(misc, lambda t: x2_n[:, t, :], ident).then_inc(misc_written, 1)
                if name == "lg":
                    take_misc(it, (s, "lg", 0))
                    for t in range(TT):
                        last = nc.tensor.matmul(misc_tok[:, t, :], h2T[:, P * t:P * (t + 1)], w_router[:, :],
                                                start=True, stop=True)
                    last.then_inc(misc_written, 1)
                if name == "ct":
                    pe.wait_ge(coef_split, it)
                    take_misc(it, (s, "ct", 0))
                    transposes(misc_bf, lambda t: coef_parts[:, t, :], ident_bf).then_inc(misc_written, 1)
                if name == "g":
                    need(pe, gate_read, it * GATE_USES + (a - GATE_USES))
                    nc.tensor.matmul(gate_bank[:, :], wg[:, P * a:P * (a + 1)], h2T[:, :], start=True,
                                     stop=True).then_inc(gate_written, 1)
                if name == "u":
                    need(pe, up_read, it * MB + (a - MB))
                    nc.tensor.matmul(up_bank[:, :], wu[:, P * a:P * (a + 1)], h2T[:, :], start=True,
                                     stop=True).then_inc(up_written, 1)
                if name == "c":
                    take_misc(it, (s, "c", a))
                    nc.tensor.matmul(misc[:, :], pick[:, a, :, :].rearrange("p a b -> p (a b)"), coef_T[:, :],
                                     start=True, stop=True).then_inc(misc_written, 1)
                if name == "down":
                    if a == 0:
                        pe.wait_ge(up_read, it * MB)
                        pe.wait_ge(weighted, it * FB)
                        pe.wait_ge(gate_read, it * GATE_USES - 1)
                    for m in range(MB):
                        last = nc.tensor.matmul(gate_bank[:, P * a:P * (a + 1)], hidden[:, m, P * a:P * (a + 1)],
                                                wd[:, m, :], start=(m == 0), stop=(m == MB - 1))
                    if a == TT - 1:
                        last.then_inc(down_written, 1)

            walk(pe, run)


_INS = ["L0_attn_x", "L0_attn_Wq", "L0_attn_bq", "L0_attn_Wk", "L0_attn_bk", "L0_attn_Wv", "L0_attn_bv",
        "L0_attn_Wo", "L0_attn_bo", "L0_attn_gamma", "L0_attn_beta", "L0_ffn_router", "L0_ffn_experts_gate",
        "L0_ffn_experts_up", "L0_ffn_experts_down", "L0_ffn_shared_gate", "L0_ffn_shared_up",
        "L0_ffn_shared_down", "L0_c", "L0_wmod"]


def kernel(**inputs):
    import numpy as np
    import concourse.bacc as bacc
    from concourse.bass_utils import run_bass_kernel_spmd

    nc = bacc.Bacc("TRN2", target_bir_lowering=False, num_devices=1)
    arrays, args = {}, []
    for name in _INS:
        a = np.ascontiguousarray(inputs[name])
        arrays[f"in_{name}"] = a
        args.append(nc.dram_tensor(f"in_{name}", a.shape, mybir.dt.from_np(a.dtype), kind="ExternalInput").ap())
    args.append(nc.dram_tensor("out_x", (B, T, C), F32, kind="ExternalOutput").ap())
    block_kernel(nc, *args)
    r = run_bass_kernel_spmd(nc, [arrays], core_ids=[0])
    return r.results[0]["out_x"]
```

```python
from contextlib import ExitStack

import numpy as np

import concourse.bass as bass
from concourse import mybir

F32 = mybir.dt.float32
BF16 = mybir.dt.bfloat16
ALU = mybir.AluOpType
ACT = mybir.ActivationFunctionType
AX_X = mybir.AxisListType.X

P = 128
B = 8
T = 512
TT = T // P
C = 128
H = 16
DH = C // H
GH = 4
G = H // GH
PARTS = 3
KROWS = PARTS * PARTS * DH
MROWS = KROWS + PARTS
SROWS = PARTS * DH
E = 8
DE = 64
FB = E * DE // P
MB = FB + 1
VC = 32
EPS = 1e-5
SCALE = DH ** -0.5
MASKED = -3.0e38

S1_UNITS = ([(h, 1, 3) for h in range(GH)] + [(h, 1, 2) for h in range(GH)]
            + [(0, 2, 1), (2, 2, 1)] + [(0, 4, 0)])
S2_UNITS = ([[(h, 0)] for h in range(GH)] + [[(h, 1), (h, 3)] for h in range(GH)]
            + [[(0, 2), (1, 2)], [(2, 2), (3, 2)]])
U1, U2 = len(S1_UNITS), len(S2_UNITS)
P_AT = {0: 0, 1: 512, 3: 896, 2: 1024}
P_LEN = 1280
PV_ORDER = [(0, 4), (1, 8), (3, 8), (2, 10)]

EXTRA = {
    0: {0: [("xin", "next"), ("xs", "next")], 2: [("mod0", "first"), ("uev", "")], 3: [("xn", "next")],
        4: [("xres", "prev")], 6: [("o", "")], 10: [("msplit", "cur"), ("xt", "next")],
        13: [("max", "cur")]},
    1: {0: [("q", "next")], 2: [("uev", "")], 3: [("mod1", "first"), ("k", "next"), ("vaug", "cur")],
        5: [("o", "")], 7: [("stack", "next"), ("ot", "prev")],
        8: [("y", "prev"), ("ystat", "prev"), ("mod2", "first")], 9: [("yn", "prev"), ("mod3", "first")],
        10: [("msplit", "cur")], 11: [("x2", "prev"), ("mod4", "first")], 12: [("max", "cur")],
        13: [("x2stat", "prev")], 14: [("v", "next")]},
    2: {0: [("x2n", "prev")], 2: [("uev", ""), ("x2t", "prev")],
        5: [("g0", "prev"), ("lg", "prev"), ("route", "prev"), ("prob", "prev")],
        7: [("u0", "prev"), ("above", "prev")], 8: [("rank", "prev"), ("g1", "prev")], 9: [("o", "")],
        11: [("u1", "prev"), ("msplit", "cur")], 13: [("g2", "prev"), ("ct", "prev"), ("u2", "prev")],
        14: [("max", "cur")]},
    3: {0: [("c0", "prev")], 2: [("c1", "prev"), ("uev", "")],
        3: [("g3", "prev"), ("c2", "prev"), ("u3", "prev")], 5: [("c3", "prev"), ("g4", "prev")],
        6: [("u4", "prev")], 9: [("o", "")], 11: [("msplit", "cur"), ("down0", "prev")],
        12: [("down1", "prev"), ("max", "cur")],
        13: [("down2", "prev"), ("down3", "prev"), ("down4", "prev")], 14: [("fin", "prev")]},
}
LAST = ["y", "ystat", "yn", "x2", "x2stat", "x2n", "x2t", "lg", "route", "prob", "above", "rank",
        "g0", "u0", "g1", "g2", "u1", "g3", "ct", "u2", "c0", "g4", "c1", "u3", "u4", "c2", "c3",
        "down0", "down1", "down2", "down3", "down4", "fin"]
PV_STEPS = [13, 1, 2, 2]
STEPS = 15
S1_STEPS = [0, 0, 2, 2, 3, 5, 5, 7, 8, 9, 10]
S2_STEPS = [4, 6, 6, 8, 8, 9, 10, 10, 12, 13]
LATER = {
    "dve": {(0, "msplit", 0): 3, (0, "o", 0): 3, (1, "o", 0): 1, (1, "x2", 0): 1, (1, "x2stat", 0): 1,
        (1, "yn", 0): 2, (2, "g", 1): 3, (2, "msplit", 0): 2, (2, "o", 0): 1, (2, "prob", 0): 2,
        (2, "u", 0): 1, (2, "u", 2): 3, (2, "x2n", 0): 1, (3, "fin", 0): 1, (3, "g", 3): 1, (3, "g", 4): 1,
        (3, "u", 3): 2, (3, "u", 4): 3},
    "pool": {(0, "xs", 0): 3, (1, "k", 0): 2, (1, "ot", 0): 1, (1, "q", 0): 2, (1, "vaug", 0): 1,
        (1, "x2stat", 0): 2, (3, "c", 0): 2, (3, "c", 3): 2},
    "act": {(0, "max", 0): 2, (0, "uev", 0): 1, (0, "xt", 0): 1, (1, "max", 0): 1, (1, "q", 0): 2,
        (1, "v", 0): 3, (2, "ct", 0): 1, (3, "c", 0): 2, (3, "max", 0): 1, (3, "uev", 0): 1},
}


def numbered(name):
    return (name[:-1], int(name[-1])) if name[-1].isdigit() and name != "x2" else (name, 0)


def slots(has_prev, has_cur, has_next, engine=None):
    live = {"prev": has_prev, "cur": has_cur, "next": has_next, "first": not has_prev}
    last = not has_cur
    later = LATER.get(engine, {})
    out = []

    def put(s, k, rank, name, a):
        at = STEPS * s + k + later.get((s, name, a), 0)
        out.append((min(at, STEPS * G - 1), rank, len(out), (s, name, a)))

    for s in range(G):
        s1 = has_cur
        s2 = has_cur if s > 0 else has_prev
        o = has_prev if s < 2 else has_cur
        if s1:
            put(s, 0, 0, "load", 0)
            for a, k in enumerate(S1_STEPS):
                put(s, k, 1, "s1", a)
        if s2:
            for a, k in enumerate(S2_STEPS):
                put(s, k, 2, "s2", a)
            put(s, PV_STEPS[0], 3, "pv", 0)
        if o:
            for a, k in enumerate(PV_STEPS[1:]):
                put(s, k, 3, "pv", a + 1)
        for k, tasks in EXTRA[s].items():
            for name, whose in tasks:
                if (o if whose == "" else live[whose]) and not (last and name in LAST):
                    put(s, k, 4, *numbered(name))
    out = [x[-1] for x in sorted(out)]
    if last:
        out += [(G - 1, *numbered(name)) for name in LAST]
    return out


PROLOGUE = [(0, *numbered(name)) for name in (
    "xin", "xs", "cond", "xn", "late", "xt", "gates0", "q", "gates1", "k", "gates2", "stack", "v", "gates3")]
KINDS = {-1: PROLOGUE, 0: slots(False, True, True), 1: slots(True, True, True),
         B - 1: slots(True, True, False), B: slots(True, False, False)}
LOOP = (1, B - 1)

MISC_TASKS = ("o", "ot", "y", "x2t", "lg", "ct", "c", "xt", "q", "k", "v", "max")


def misc_uses(kind):
    return [x for x in KINDS[kind] if x[1] in MISC_TASKS]


def s_of(it, task):
    return next(s for s, name, _ in KINDS[it if isinstance(it, int) else 1] if name == task)


def misc_at(it, task):
    before = len(misc_uses(-1))
    if isinstance(it, int) and it <= 0:
        return (before if it == 0 else 0) + misc_uses(it).index(task)
    before += len(misc_uses(0))
    each = len(misc_uses(1))
    if isinstance(it, int) and it >= LOOP[1]:
        before += (LOOP[1] - 1) * each + (len(misc_uses(B - 1)) if it == B else 0)
        return before + misc_uses(it).index(task)
    return it * each + (before - each + misc_uses(1).index(task))


def need(eng, sem, value):
    if not isinstance(value, int) or value > 0:
        eng.wait_ge(sem, value)


def need_all(eng, const, *waits):
    waits = [(m, v if isinstance(v, int) else eng.to_reg(v)) for m, v in waits]
    eng.wait_ge(*const)
    for m, v in waits:
        need(eng, m, v)


def walk(eng, engine, run):
    for task in PROLOGUE:
        run(-1, *task)
    for task in slots(False, True, True, engine):
        run(0, *task)
    with eng.Fori(*LOOP) as it:
        for task in slots(True, True, True, engine):
            run(it, *task)
    for task in slots(True, True, False, engine):
        run(B - 1, *task)
    for task in slots(True, False, False, engine):
        run(B, *task)


def block_kernel(nc, x, Wq, bq, Wk, bk, Wv, bv, Wo, bo, gamma, beta, router, w_gate, w_up, w_down,
                 sh_gate, sh_up, sh_down, cond, wmod, out):
    q_scr = nc.dram_tensor("q_scr", [P, PARTS, T], BF16, kind="Internal").ap()
    k_scr = [nc.dram_tensor(f"k_scr{r}", [P, PARTS, T], BF16, kind="Internal").ap()
             for r in range(PARTS)]

    with ExitStack() as ctx:
        def sb(name, shape, dt=F32):
            return ctx.enter_context(nc.sbuf_tensor(name, shape, dt))

        def bank(name):
            return ctx.enter_context(nc.psum_tensor(name, [P, 512], F32))

        def sem(name):
            return ctx.enter_context(nc.semaphore(name))

        s1_bank = [bank("s1_bank0"), bank("s1_bank1")]
        s2_bank = [bank("s2_bank0"), bank("s2_bank1")]
        pv_bank, misc, gate_bank, up_bank = (bank(x) for x in ("pv_bank", "misc", "gate_bank", "up_bank"))
        misc_tok = misc[:, :].rearrange("p (t c) -> p t c", t=TT)
        misc_bf = misc[:, :].bitcast(BF16)

        wq, wk, wv, wo = (sb(x, [P, C]) for x in ("wq", "wk", "wv", "wo"))
        wg, wu = sb("wg", [P, MB * P]), sb("wu", [P, MB * P])
        wd = sb("wd", [P, MB, C])
        w_router = sb("w_router", [P, P])
        bq_col, bk_col = sb("bq_col", [P, 1]), sb("bk_col", [P, 1])
        bv_row, bo_row, gamma_row, beta_row = (sb(x, [P, C]) for x in ("bv_row", "bo_row", "gamma_row", "beta_row"))
        wmod_sb = sb("wmod_sb", [P, 6 * C])
        cond_sb, cond_t, cond_s = (sb(x, [B, P]) for x in ("cond_sb", "cond_t", "cond_s"))
        cond_T = sb("cond_T", [P, B])
        cond_rep = sb("cond_rep", [P, B, P])
        mod_cols = sb("mod_cols", [P, 4, B])
        gate_a, gate_b = sb("gate_a", [P, B, C]), sb("gate_b", [P, B, C])
        gate_sign, gate_abs = sb("gate_sign", [P, B, C]), sb("gate_abs", [P, B, C])
        gamma_a, beta_a = sb("gamma_a", [P, B, C]), sb("beta_a", [P, B, C])
        ident, ident_bf = sb("ident", [P, P]), sb("ident_bf", [P, P], BF16)
        causal = sb("causal", [P, P], BF16)
        pick = sb("pick", [P, FB, 2, DE], BF16)
        earlier = sb("earlier", [P, E, E])
        neg_half = sb("neg_half", [P, TT])
        zero_row = sb("zero_row", [1, 512], BF16)
        x_in, x_n = sb("x_in", [P, TT, C]), sb("x_n", [P, TT, C])
        h1T = sb("h1T", [P, T])
        q_parts, k_parts = sb("q_parts", [P, PARTS, T], BF16), sb("k_parts", [P, PARTS, T], BF16)
        q_rest, k_rest = sb("q_rest", [P, T]), sb("k_rest", [P, T])
        v_tok = sb("v_tok", [P, TT, C])
        q_stack, k_stack = sb("q_stack", [P, H, T], BF16), sb("k_stack", [P, H, T], BF16)
        v_aug = sb("v_aug", [P, TT, H, VC])
        row_max = [sb(f"row_max{i}", [P, GH, TT]) for i in range(2)]
        max_parts = sb("max_parts", [P, PARTS, GH * TT], BF16)
        max_rest = sb("max_rest", [P, GH * TT])
        max_rows = sb("max_rows", [PARTS * GH * TT, P], BF16)
        probs = [sb(f"probs{i}", [P, GH, P_LEN]) for i in range(2)]
        u_sb = sb("u_sb", [P, T])
        denom = sb("denom", [P, TT * GH])
        o_tok = sb("o_tok", [P, TT, C])
        oT = sb("oT", [P, T])
        x_res, y_sb, x2, x2_n = (sb(x, [P, TT, C]) for x in ("x_res", "y_sb", "x2", "x2_n"))
        h2T = sb("h2T", [P, T])
        stats = {k: sb(f"stats_{k}", [P, TT, 6]) for k in ("x", "y", "x2")}
        mean_var = {k: sb(f"mean_var_{k}", [P, TT, 2]) for k in ("x", "y", "x2")}
        var_eps = {k: sb(f"var_eps_{k}", [P, TT]) for k in ("x", "y", "x2")}
        rstd = {k: sb(f"rstd_{k}", [P, TT]) for k in ("x", "y", "x2")}
        lmax, esum, erec = (sb(x, [P, TT]) for x in ("lmax", "esum", "erec"))
        logit, expo, prob, rank, coef, coef_rest = (
            sb(x, [P, TT, E]) for x in ("logit", "expo", "prob", "rank", "coef", "coef_rest"))
        above, equal = sb("above", [P, TT, E, E]), sb("equal", [P, TT, E, E])
        coef_parts = sb("coef_parts", [P, TT, P], BF16)
        coef_T = sb("coef_T", [P, T], BF16)
        tanh_sb, silu_sb = sb("tanh_sb", [P, T]), sb("silu_sb", [P, T])
        hidden = sb("hidden", [P, MB, T])
        coef_sb = sb("coef_sb", [P, T])
        ffn_sb, out_sb = sb("ffn_sb", [P, TT, C]), sb("out_sb", [P, TT, C])

        qkv_in = sem("qkv_in")
        rows_in = sem("rows_in")
        ffn_in = sem("ffn_in")
        cond_in = sem("cond_in")
        const_step = sem("const_step")
        const_done = sem("const_done")
        minus_ones = sem("minus_ones")
        ct_step = sem("ct_step")
        cond_mm = sem("cond_mm")
        gates_read = sem("gates_read")
        vec_setup = sem("vec_setup")
        x_in_ready, x_stats, x_mv = sem("x_in_ready"), sem("x_stats"), sem("x_mv")
        x_ve, x_rstd, x_norm = sem("x_ve"), sem("x_rstd"), sem("x_norm")
        q_first, k_first = sem("q_first"), sem("k_first")
        q_second, k_second, q_split, k_split = (sem(x) for x in ("q_second", "k_second", "q_split", "k_split"))
        scr_written = sem("scr_written")
        first_written = sem("first_written")
        misc_written, misc_read = sem("misc_written"), sem("misc_read")
        stacked = [sem(f"stacked{g}") for g in range(G)]
        s1_written, s1_reduced = sem("s1_written"), sem("s1_reduced")
        s2_written, exp_done, probs_ready = sem("s2_written"), sem("exp_done"), sem("probs_ready")
        max_step, max_landed = sem("max_step"), sem("max_landed")
        pv_done, u_ready, denom_ready, v_ready = (sem(x) for x in ("pv_done", "u_ready", "denom_ready", "v_ready"))
        xres_in, xres_ready = sem("xres_in"), sem("xres_ready")
        y_stats, y_mv, y_ve, y_rstd = (sem(x) for x in ("y_stats", "y_mv", "y_ve", "y_rstd"))
        x2_stats, x2_mv, x2_ve, x2_rstd, x2_norm = (
            sem(x) for x in ("x2_stats", "x2_mv", "x2_ve", "x2_rstd", "x2_norm"))
        y_norm, y_scaled, x2_ready = sem("y_norm"), sem("y_scaled"), sem("x2_ready")
        lmax_ready, expo_ready = sem("lmax_ready"), sem("expo_ready")
        route_step, coef_ready, coef_step, coef_split = (
            sem(x) for x in ("route_step", "coef_ready", "coef_step", "coef_split"))
        weighted = sem("weighted")
        gate_written, tanh_ready, gate_read = sem("gate_written"), sem("tanh_ready"), sem("gate_read")
        up_written, up_read = sem("up_written"), sem("up_read")
        down_written, ffn_gated, out_ready, stored = (
            sem(x) for x in ("down_written", "ffn_gated", "out_ready", "stored"))
        block = ctx.enter_context(nc.Block())

        QKV_DMAS, ROW_DMAS, FFN_DMAS = 5, 4, 11
        Q_DMAS = 2 * PARTS
        SCR_DMAS = 1 + 1 + 2 * (PARTS - 1)
        GATE_USES = MB + 1
        ROUTE_STEPS = 8

        def tok(dram, b):
            return dram[b].rearrange("(t p) c -> p t c", p=P)

        def over_tiles(row):
            return row.unsqueeze(1).to_broadcast([P, TT, C])

        def first(it):
            return isinstance(it, int) and it == -1

        def last(it):
            return isinstance(it, int) and it == B

        def gate_of(it, a):
            return s1_bank[0] if last(it) and a % 2 else gate_bank

        def up_of(it, a):
            return s1_bank[1] if last(it) and a % 2 else up_bank

        def silu_of(it, a):
            return coef_sb if last(it) and a % 2 else silu_sb

        def down_of(it):
            return s2_bank[0] if last(it) else gate_bank

        @block.sync
        def _(sp):
            sp.dma_start(cond_sb[:, :], cond).then_inc(cond_in, 16)
            sp.dma_start(wmod_sb[:, :], wmod).then_inc(cond_in, 16)
            sp.dma_start(x_in[:, :, :], tok(x, 0)).then_inc(x_in_ready, 16)
            for dst, src in ((wq, Wq), (wk, Wk), (wv, Wv)):
                sp.dma_start(dst[:, :], src).then_inc(qkv_in, 16)
            sp.dma_start(bq_col[:, :], bq.unsqueeze(1)).then_inc(qkv_in, 16)
            sp.dma_start(bk_col[:, :], bk.unsqueeze(1)).then_inc(qkv_in, 16)

            def load_stacks(it, g, written=scr_written):
                need(sp, s2_written, it * (G * U2) + U2 * (g + 1 - G))
                need(sp, written, it * (16 * SCR_DMAS) + 16 * SCR_DMAS)
                heads = slice(GH * g, GH * g + GH)
                for r in range(PARTS):
                    rows = slice(SROWS * r, SROWS * (r + 1))
                    for stack, scr in ((q_stack, q_scr), (k_stack, k_scr[r])):
                        src = scr.rearrange("(h d) s t -> (d s) h t", d=DH)
                        sp.dma_start(stack[rows, heads, :], src[:, heads, :]).then_inc(stacked[g], 16)

            def run(it, s, name, a):
                if name == "xres":
                    need(sp, x2_ready, it - 1)
                    sp.dma_start(x_res[:, :, :], tok(x, it - 1)).then_inc(xres_in, 16)
                if name == "stack":
                    sp.wait_ge(const_done, 1)
                    for g in range(G):
                        need(sp, stacked[g], it * (16 * Q_DMAS) + 16 * Q_DMAS)
                    for rows, done in (((slice(0, P // G), first_written), (slice(P // G, P), scr_written))
                                       if first(it) else ((slice(0, P), scr_written),)):
                        sp.wait_ge(q_split, it + 2)
                        sp.dma_start(q_scr[rows], q_parts[rows]).then_inc(done, 16)
                        sp.wait_ge(k_split, it + 2)
                        sp.dma_start(k_scr[0][rows], k_parts[rows]).then_inc(done, 16)
                        for r in range(1, PARTS):
                            sp.dma_start(k_scr[r][rows, 0:PARTS - r, :], k_parts[rows, r:PARTS, :]).then_inc(done, 16)
                            sp.dma_start(k_scr[r][rows, PARTS - r:PARTS, :], k_parts[rows, 0:r, :]).then_inc(done, 16)
                        if done is first_written:
                            sp.wait_ge(minus_ones, 1)
                            load_stacks(0, 0, first_written)
                    if isinstance(it, int) and it < 0:
                        load_stacks(0, 1)
                if name == "load" and s < 2:
                    load_stacks(it, s + 2)
                if name == "load" and s >= 2 and has_next(it):
                    load_stacks(it + 1, s - 2)
                if name == "fin":
                    sp.wait_ge(out_ready, it)
                    sp.dma_start(tok(out, it - 1), out_sb[:, :, :]).then_inc(stored, 16)

            def has_next(it):
                return not isinstance(it, int) or it < B - 1

            walk(sp, "sp", run)
            sp.wait_ge(stored, 16 * B)

        @block.gpsimd
        def _(pool):
            nc.gpsimd.memset(ident[:, :], 0.0)
            nc.gpsimd.memset(neg_half[:, :], -0.5)
            nc.gpsimd.memset(zero_row[:, :], 0.0)
            nc.gpsimd.memset(ident_bf[:, :], 0.0)
            nc.gpsimd.memset(w_router[:, :], 0.0)
            nc.gpsimd.memset(causal[:, :], 0.0).then_inc(const_step, 1)
            pool.wait_ge(const_step, 1)
            for m in (ident, ident_bf):
                final = nc.gpsimd.affine_select(out=m[:, :], in_=m[:, :], compare_op=ALU.not_equal, fill=1.0,
                                               base=0, pattern=[[-1, P]], channel_multiplier=1)
            final = nc.gpsimd.affine_select(out=causal[:, :], in_=causal[:, :], compare_op=ALU.is_ge, fill=MASKED,
                                           base=0, pattern=[[-1, P]], channel_multiplier=1)
            final.then_inc(const_done, 1)

            def late_constants():
                nc.gpsimd.memset(pick[:, :, :, :], 0.0)
                nc.gpsimd.memset(earlier[:, :, :], 1.0)
                nc.gpsimd.memset(coef_parts[:, :, :], 0.0)
                nc.gpsimd.memset(v_aug[:, :, :, :], 0.0).then_inc(const_step, 1)
                pool.wait_ge(const_step, 2)
                nc.gpsimd.memset(v_aug[:, :, :, DH:DH + 1], 1.0)
                nc.gpsimd.affine_select(out=earlier[:, :, :], in_=earlier[:, :, :], compare_op=ALU.is_ge, fill=0.0,
                                        base=-1, pattern=[[1, E], [-1, E]], channel_multiplier=0).then_inc(const_step, 1)
                for part in range(PARTS):
                    pool.wait_ge(const_step, 3 + part)
                    nc.gpsimd.affine_select(out=pick[:, :, :, :], in_=pick[:, :, :, :], compare_op=ALU.not_equal,
                                            fill=1.0, base=-part * E, pattern=[[-2, FB], [-1, 2], [0, DE]],
                                            channel_multiplier=1).then_inc(const_step, 1)
                pool.wait_ge(const_step, 3 + PARTS)

            def inv_std(key, mv_sem, ve_sem, rstd_sem, b1):
                need_all(pool, (const_done, 1), (mv_sem, b1))
                nc.gpsimd.tensor_scalar(var_eps[key][:, :], mean_var[key][:, :, 1], EPS, None, ALU.add).then_inc(ve_sem, 1)
                pool.wait_ge(ve_sem, b1)
                nc.gpsimd.tensor_tensor(rstd[key][:, :], var_eps[key][:, :], neg_half[:, :], ALU.pow).then_inc(rstd_sem, 1)

            def split_rest(it, name, parts, rest, second, done):
                need_all(pool, (const_done, 1), (misc_read, misc_at(it, name) + 1), (scr_written, it * (16 * SCR_DMAS) + 16 * SCR_DMAS))
                nc.gpsimd.tensor_scalar(parts[:, 1, :], rest[:, :], 1.0, None, ALU.mult).then_inc(second, 1)
                pool.wait_ge(second, it + 2)
                nc.gpsimd.tensor_tensor(parts[:, 2, :], rest[:, :], parts[:, 1, :], ALU.subtract).then_inc(done, 1)

            def run(it, s, name, a):
                if name == "xs":
                    inv_std("x", x_mv, x_ve, x_rstd, it + 2)
                if name == "xn" and not first(it):
                    need_all(pool, (const_done, 1), (x_rstd, it + 2))
                    for t in range(TT):
                        final = nc.gpsimd.tensor_scalar(x_n[:, t, :], x_in[:, t, :], mean_var["x"][:, t, 0:1],
                                                       rstd["x"][:, t:t + 1], ALU.subtract, ALU.mult)
                    final.then_inc(x_norm, 1)
                if name == "late":
                    late_constants()
                if name == "vaug":
                    need(pool, pv_done, it * G)
                    pool.wait_ge(misc_read, misc_at(it, misc_uses(it if isinstance(it, int) else 1)[0]))
                    pool.wait_ge(rows_in, 16 * ROW_DMAS)
                    nc.gpsimd.tensor_tensor(
                        v_aug[:, :, :, 0:DH], v_tok[:, :, :].rearrange("p t (h d) -> p t h d", h=H),
                        bv_row[:, :].rearrange("p (h d) -> p h d", h=H).unsqueeze(1).to_broadcast([P, TT, H, DH]),
                        ALU.add).then_inc(v_ready, 1)
                if name == "yn" and not last(it):
                    pool.wait_ge(y_norm, it)
                    nc.gpsimd.tensor_tensor(y_sb[:, :, :], y_sb[:, :, :], over_tiles(gamma_a[:, it - 1, :]),
                                            ALU.mult).then_inc(y_scaled, 1)
                if name == "c" and not last(it):
                    pool.wait_ge(misc_read, misc_at(it, (s, "c", a)) + 1)
                    pool.wait_ge(up_read, it * MB + (a + 1 - MB))
                    nc.gpsimd.tensor_tensor(hidden[:, a, :], hidden[:, a, :], coef_sb[:, :], ALU.mult).then_inc(weighted, 1)
                if name == "fin" and not last(it):
                    pool.wait_ge(gate_read, it * GATE_USES)
                    need(pool, stored, it * 16 - 16)
                    nc.gpsimd.tensor_tensor(out_sb[:, :, :], ffn_sb[:, :, :], x2[:, :, :], ALU.add).then_inc(out_ready, 1)
                if name == "q" and not first(it):
                    split_rest(it, (s, "q", 0), q_parts, q_rest, q_second, q_split)
                if name == "k" and not first(it):
                    split_rest(it, (s, "k", 0), k_parts, k_rest, k_second, k_split)
                if name == "s2":
                    ng = (s - 1) % G
                    pr = probs[ng % 2]
                    need_all(pool, (const_done, 1), (exp_done, it * (G * U2) + U2 * (s - 1) + a + 1))
                    h, j = S2_UNITS[a][0]
                    if a < 4:
                        view, pat = pr[:, h, P_AT[0]:P_AT[0] + P], [[1, P]]
                    elif a < 8:
                        at = P_AT[1]
                        step = P_AT[3] - P_AT[1]
                        view = pr[:, h, at:at + 2 * step].rearrange("p (a b) -> p a b", a=2)[:, :, 0:P]
                        pat = [[0, 2], [1, P]]
                    else:
                        view, pat = pr[:, h:h + 2, P_AT[2]:P_AT[2] + P], [[0, 2], [1, P]]
                    nc.gpsimd.affine_select(out=view, in_=view, compare_op=ALU.is_ge, fill=0.0, base=0,
                                            pattern=pat, channel_multiplier=-1).then_inc(probs_ready, 1)
                if name == "ystat":
                    inv_std("y", y_mv, y_ve, y_rstd, it)
                if name == "x2stat":
                    inv_std("x2", x2_mv, x2_ve, x2_rstd, it)
                if name == "ot":
                    pool.wait_ge(xres_in, it * 16)
                    pool.wait_ge(vec_setup, 1)
                    nc.gpsimd.tensor_tensor(x_res[:, :, :], x_res[:, :, :], over_tiles(beta_a[:, it - 1, :]),
                                            ALU.add).then_inc(xres_ready, 1)
                if name == "rank":
                    c = coef[:, :, :]
                    cp = [coef_parts[:, :, E * k:E * k + E] for k in range(PARTS)]
                    need_all(pool, (const_done, 1), (coef_ready, it))
                    nc.gpsimd.tensor_scalar(cp[0], c, 1.0, None, ALU.mult).then_inc(coef_step, 1)
                    pool.wait_ge(coef_step, it * 3 - 2)
                    nc.gpsimd.tensor_tensor(coef_rest[:, :, :], c, cp[0], ALU.subtract).then_inc(coef_step, 1)
                    need_all(pool, (const_done, 1), (coef_step, it * 3 - 1))
                    nc.gpsimd.tensor_scalar(cp[1], coef_rest[:, :, :], 1.0, None, ALU.mult).then_inc(coef_step, 1)
                    pool.wait_ge(coef_step, it * 3)
                    nc.gpsimd.tensor_tensor(cp[2], coef_rest[:, :, :], cp[1], ALU.subtract).then_inc(coef_split, 1)

            walk(pool, "pool", run)

        @block.scalar
        def _(act):
            act.wait_ge(cond_in, 32)
            nc.scalar.activation(cond_t[:, :], cond_sb[:, :], ACT.Tanh, scale=0.5).then_inc(ct_step, 1)
            for dst, src in ((bv_row, bv), (gamma_row, gamma), (beta_row, beta), (bo_row, bo)):
                act.dma_start(dst[:, :], src.unsqueeze(0).to_broadcast([P, C])).then_inc(rows_in, 16)
            act.dma_start(wo[:, :], Wo).then_inc(ffn_in, 16)
            act.wait_ge(const_done, 1)
            act.dma_start(w_router[:, 0:E], router).then_inc(ffn_in, 16)
            for dst, experts, shared in ((wg, w_gate, sh_gate), (wu, w_up, sh_up)):
                act.dma_start(dst[:, 0:FB * P].rearrange("p (e d) -> p e d", e=E),
                              experts.rearrange("e h d -> h e d")).then_inc(ffn_in, 16)
                act.dma_start(dst[:, FB * P:MB * P], shared).then_inc(ffn_in, 16)
            for m in range(FB):
                act.dma_start(wd[:, m, :], w_down[2 * m:2 * m + 2].rearrange("e d h -> (e d) h")).then_inc(ffn_in, 16)
            act.dma_start(wd[:, FB, :], sh_down).then_inc(ffn_in, 16)
            act.wait_ge(ct_step, 6)
            act.wait_ge(qkv_in, 16 * QKV_DMAS)

            def part_first(it, name, col, parts, first):
                act.wait_ge(misc_written, misc_at(it, name) + 1)
                need(act, scr_written, it * (16 * SCR_DMAS) + 16 * SCR_DMAS)
                nc.scalar.activation(parts[:, 0, :], misc[:, :], ACT.Identity, bias=col[:, 0:1]).then_inc(first, 1)

            def run(it, s, name, a):
                if name == "xin" and not (isinstance(it, int) and it == -1):
                    need(act, x_norm, it + 1)
                    act.dma_start(x_in[:, :, :], tok(x, it + 1)).then_inc(x_in_ready, 16)
                if name == "xt":
                    act.wait_ge(misc_written, misc_at(it, (s, "xt", 0)) + 1)
                    nc.scalar.activation(h1T[:, :], misc[:, :], ACT.Identity, scale=mod_cols[:, 1, it + 1].unsqueeze(1),
                                         bias=mod_cols[:, 0, it + 1].unsqueeze(1)).then_inc(misc_read, 1)
                if name == "q":
                    part_first(it, (s, "q", 0), bq_col, q_parts, q_first)
                if name == "k":
                    part_first(it, (s, "k", 0), bk_col, k_parts, k_first)
                if name == "v":
                    act.wait_ge(misc_written, misc_at(it, (s, "v", 0)) + 1)
                    need(act, v_ready, it + 1)
                    nc.scalar.activation(v_tok[:, :, :], misc_tok, ACT.Copy).then_inc(misc_read, 1)
                if name == "s2":
                    pr = probs[(s - 1) % G % 2]
                    u = U2 * (s - 1) + a
                    act.wait_ge(s2_written, it * (G * U2) + (u + 1))
                    h, j = S2_UNITS[a][0]
                    src = s2_bank[u % 2][:, :]
                    if a < 8:
                        at = P_AT[j]
                        dst = pr[:, h, at:at + 512]
                    else:
                        dst = pr[:, h:h + 2, P_AT[2]:P_AT[2] + 256]
                        src = src.rearrange("p (a b) -> p a b", a=2)
                    nc.scalar.activation(dst, src, ACT.Exp, scale=SCALE).then_inc(exp_done, 1)
                if name == "uev":
                    act.wait_ge(pv_done, it * G + (s - 1))
                    if not (isinstance(it, int) and (it, s) == (0, 2)):
                        if s > 0:
                            act.wait_ge(misc_written, misc_at(it, (s - 1, "o", 0)) + 1)
                        else:
                            act.wait_ge(misc_written, misc_at(it, misc_uses(it if isinstance(it, int) else 1)[0]))
                    nc.scalar.activation(u_sb[:, :], pv_bank[:, :], ACT.Copy).then_inc(u_ready, 1)
                if name == "max":
                    k = misc_at(it, (s, "max", 0)) + 1
                    act.wait_ge(misc_written, k)
                    need(act, max_landed, it * (16 * G) + 16 * s)
                    nc.scalar.activation(max_rows[:, :], misc_bf[0:PARTS * GH * TT, 0:P], ACT.Copy).then_inc(misc_read, 1)
                    act.wait_ge(misc_read, k)
                    act.dma_start(q_stack[KROWS:MROWS, GH * s:GH * s + GH, :].rearrange("p h (b t) -> p (h b) t", t=P),
                                  max_rows[:, :]).then_inc(max_landed, 16)
                if name == "ot":
                    act.wait_ge(misc_written, misc_at(it, (s, "ot", 0)) + 1)
                    nc.scalar.activation(oT[:, :], misc[:, :], ACT.Copy).then_inc(misc_read, 1)
                if name == "x2t":
                    act.wait_ge(misc_written, misc_at(it, (s, "x2t", 0)) + 1)
                    nc.scalar.activation(h2T[:, :], misc[:, :], ACT.Identity, scale=mod_cols[:, 3, it - 1].unsqueeze(1),
                                         bias=mod_cols[:, 2, it - 1].unsqueeze(1)).then_inc(misc_read, 1)
                if name == "route":
                    act.wait_ge(misc_read, misc_at(it, (s_of(it, "lg"), "lg", 0)) + 1)
                    nc.scalar.activation(expo[:, :, :], logit[:, :, :], ACT.Exp).then_inc(expo_ready, 1)
                if name == "ct":
                    act.wait_ge(misc_written, misc_at(it, (s, "ct", 0)) + 1)
                    nc.scalar.activation(coef_T[:, :], misc_bf[:, 0:T], ACT.Copy).then_inc(misc_read, 1)
                if name == "c" and not last(it):
                    act.wait_ge(misc_written, misc_at(it, (s, "c", a)) + 1)
                    need(act, weighted, it * FB + (a - FB))
                    nc.scalar.activation(coef_sb[:, :], misc[:, :], ACT.Copy).then_inc(misc_read, 1)
                if name == "g":
                    act.wait_ge(gate_written, it * MB + (a + 1 - MB))
                    if a > 0:
                        act.wait_ge(gate_read, it * GATE_USES + (a - GATE_USES))
                    nc.scalar.activation(tanh_sb[:, :], gate_of(it, a)[:, :], ACT.Tanh, scale=0.5).then_inc(tanh_ready, 1)

            walk(act, "act", run)

        @block.vector
        def _(dve):
            nc.vector.memset(k_stack[64:MROWS, :, :].rearrange("p h t -> p (h t)").bitcast(F32),
                             float(np.array([0xBF80BF80], np.uint32).view(np.float32)[0])).then_inc(minus_ones, 1)

            def condition():
                dve.wait_ge(ct_step, 1)
                nc.vector.scalar_tensor_tensor(cond_s[:, :], cond_t[:, :], 1.0, cond_sb[:, :], ALU.add,
                                               ALU.mult).then_inc(ct_step, 1)
                dve.wait_ge(cond_mm, 1)
                nc.vector.tensor_scalar(cond_T[:, :], pv_bank[:, 0:B], 0.5, None, ALU.mult).then_inc(ct_step, 1)
                dve.wait_ge(cond_mm, 2)
                nc.vector.tensor_copy(mod_cols[:, 0::2, :], up_bank[:, 0:2 * B].rearrange("p (j b) -> p j b", j=2)).then_inc(ct_step, 1)
                nc.vector.tensor_scalar(mod_cols[:, 1::2, :], up_bank[:, 2 * B:4 * B].rearrange("p (j b) -> p j b", j=2),
                                        1.0, None, ALU.add).then_inc(ct_step, 1)
                dve.wait_ge(ct_step, 5)
                nc.vector.tensor_copy(cond_rep[:, :, :], cond_T[:, :].unsqueeze(2).to_broadcast([P, B, P])).then_inc(ct_step, 1)

            def gates(i):
                dve.wait_ge(cond_mm, 3 + i)
                gate, banks = ((gate_a, s1_bank), (gate_b, s2_bank))[i // 2]
                half = B // 2
                nc.vector.tensor_copy(gate[:, half * (i % 2):half * (i % 2 + 1), :],
                                      banks[i % 2][:, 0:half * C].rearrange("p (b c) -> p b c", b=half)).then_inc(gates_read, 1)

            def modulation(i):
                gate, at = (gate_a, gate_b)[i // 2 % 2], 6 + 4 * (i // 2)
                if i == 0:
                    dve.wait_ge(gates_read, 4)
                if i < 4:
                    dve.wait_ge(ct_step, 6 + 2 * i)
                if i in (0, 2):
                    nc.vector.tensor_scalar(gate_sign[:, :, :], gate[:, :, :], 0.0, 2.0, ALU.is_ge, ALU.mult).then_inc(ct_step, 1)
                    dve.wait_ge(ct_step, at + 1)
                    nc.vector.tensor_scalar(gate_sign[:, :, :], gate_sign[:, :, :], -1.0, None, ALU.add).then_inc(ct_step, 1)
                if i in (1, 3):
                    nc.vector.tensor_tensor(gate_abs[:, :, :], gate[:, :, :], gate_sign[:, :, :], ALU.mult).then_inc(ct_step, 1)
                    dve.wait_ge(ct_step, at + 3)
                    nc.vector.scalar_tensor_tensor(gate[:, :, :], gate_abs[:, :, :], 0.25, gate_sign[:, :, :], ALU.max,
                                                   ALU.mult).then_inc(ct_step, 1)
                if i == 4:
                    dve.wait_ge(rows_in, 16 * ROW_DMAS)
                    dve.wait_ge(ct_step, 14)
                    nc.vector.tensor_tensor(gamma_a[:, :, :], gate_a[:, :, :],
                                            gamma_row[:, :].unsqueeze(1).to_broadcast([P, B, C]), ALU.mult)
                    nc.vector.tensor_tensor(beta_a[:, :, :], gate_a[:, :, :],
                                            beta_row[:, :].unsqueeze(1).to_broadcast([P, B, C]), ALU.mult).then_inc(vec_setup, 1)
                    dve.wait_ge(vec_setup, 1)

            def layer_stats(key, src, st_sem, mv_sem, b1):
                for t in range(TT):
                    final = nc.vector.bn_stats(stats[key][:, t, :], src[:, t, :])
                final.then_inc(st_sem, 1)
                need_all(dve, (const_done, 1), (st_sem, b1))
                for t in range(TT):
                    final = nc.vector.bn_aggr(mean_var[key][:, t, :], stats[key][:, t, :])
                final.then_inc(mv_sem, 1)

            def normalise(key, dst, src, rstd_sem, norm_sem, b1):
                dve.wait_ge(rstd_sem, b1)
                for t in range(TT):
                    final = nc.vector.tensor_scalar(dst[:, t, :], src[:, t, :], mean_var[key][:, t, 0:1],
                                                   rstd[key][:, t:t + 1], ALU.subtract, ALU.mult)
                final.then_inc(norm_sem, 1)

            def rest_of(it, name, col, parts, rest, part_ready, split):
                dve.wait_ge(part_ready, it + 2)
                need(dve, split, it + 1)
                if first(it):
                    dve.wait_ge(qkv_in, 16 * QKV_DMAS)
                nc.vector.scalar_tensor_tensor(rest[:, :], misc[:, :], col[:, 0:1], parts[:, 0, :], ALU.add,
                                               ALU.subtract).then_inc(misc_read, 1)
                if first(it):
                    second = q_second if name == "q" else k_second
                    dve.wait_ge(misc_read, misc_at(it, (0, name, 0)) + 1)
                    nc.vector.tensor_copy(parts[:, 1, :], rest[:, :]).then_inc(second, 1)
                    dve.wait_ge(second, 1)
                    nc.vector.tensor_tensor(parts[:, 2, :], rest[:, :], parts[:, 1, :], ALU.subtract).then_inc(split, 1)

            def run(it, s, name, a):
                if name == "xs":
                    dve.wait_ge(x_in_ready, it * 16 + 32)
                    layer_stats("x", x_in, x_stats, x_mv, it + 2)
                if name == "cond":
                    condition()
                if name == "gates":
                    gates(a)
                if name == "mod":
                    modulation(a)
                if name == "xn" and first(it):
                    normalise("x", x_n, x_in, x_rstd, x_norm, 1)
                if name == "q":
                    rest_of(it, name, bq_col, q_parts, q_rest, q_first, q_split)
                if name == "k":
                    rest_of(it, name, bk_col, k_parts, k_rest, k_first, k_split)
                if name == "s1":
                    u = U1 * s + a
                    h, nh, qt = S1_UNITS[a]
                    dve.wait_ge(s1_written, it * (G * U1) + (u + 1))
                    if a == 0:
                        need(dve, max_step, it * (G * 4) + 4 * (s - 1))
                    w = P * (qt + 1)
                    nc.vector.reduce_max(row_max[s % 2][:, h:h + nh, qt],
                                         s1_bank[u % 2][:, 0:nh * w].rearrange("p (h k) -> p h k", h=nh),
                                         AX_X).then_inc(s1_reduced, 1)
                if name == "msplit":
                    rm = row_max[s % 2][:, :, :].rearrange("p h t -> p (h t)")
                    n4, c4 = it * (G * 4), 4 * s
                    need(dve, max_landed, it * (16 * G) + 16 * s)
                    dve.wait_ge(s1_reduced, it * (G * U1) + U1 * (s + 1))
                    nc.vector.tensor_copy(max_parts[:, 0, :], rm).then_inc(max_step, 1)
                    dve.wait_ge(max_step, n4 + (c4 + 1))
                    nc.vector.tensor_tensor(max_rest[:, :], rm, max_parts[:, 0, :], ALU.subtract).then_inc(max_step, 1)
                    dve.wait_ge(max_step, n4 + (c4 + 2))
                    nc.vector.tensor_copy(max_parts[:, 1, :], max_rest[:, :]).then_inc(max_step, 1)
                    dve.wait_ge(max_step, n4 + (c4 + 3))
                    nc.vector.tensor_tensor(max_parts[:, 2, :], max_rest[:, :], max_parts[:, 1, :],
                                            ALU.subtract).then_inc(max_step, 1)
                if name == "o":
                    g = (s - 2) % G
                    dve.wait_ge(misc_written, misc_at(it, (s, "o", 0)) + 1)
                    if g == 0 and not (isinstance(it, int) and it == 0):
                        dve.wait_ge(misc_written, misc_at(it, (s_of(it, "ot"), "ot", 0)) + 1)
                    view = misc[:, :].rearrange("p (c v) -> p c v", v=VC)
                    nc.vector.reciprocal(denom[:, :].unsqueeze(2), view[:, :, DH:DH + 1]).then_inc(denom_ready, 1)
                    dve.wait_ge(denom_ready, it * G + (s - 1))
                    nc.vector.tensor_tensor(
                        o_tok[:, :, GH * DH * g:GH * DH * (g + 1)].rearrange("p t (h d) -> p t h d", h=GH),
                        misc[:, :].rearrange("p (t h v) -> p t h v", t=TT, h=GH)[:, :, :, 0:DH],
                        denom[:, :].rearrange("p (t h) -> p t h", t=TT).unsqueeze(3).to_broadcast([P, TT, GH, DH]),
                        ALU.mult).then_inc(misc_read, 1)
                if name == "y":
                    k = misc_at(it, (s, "y", 0)) + 1
                    dve.wait_ge(misc_written, k)
                    nc.vector.tensor_tensor(y_sb[:, :, :], misc_tok, over_tiles(bo_row[:, :]), ALU.add).then_inc(misc_read, 1)
                if name == "ystat":
                    dve.wait_ge(misc_read, misc_at(it, (s_of(it, "y"), "y", 0)) + 1)
                    layer_stats("y", y_sb, y_stats, y_mv, it)
                if name == "yn":
                    normalise("y", y_sb, y_sb, y_rstd, y_norm, it)
                    if last(it):
                        dve.wait_ge(y_norm, it)
                        nc.vector.tensor_tensor(y_sb[:, :, :], y_sb[:, :, :], over_tiles(gamma_a[:, it - 1, :]),
                                                ALU.mult).then_inc(y_scaled, 1)
                if name == "x2":
                    dve.wait_ge(y_scaled, it)
                    dve.wait_ge(xres_ready, it)
                    nc.vector.tensor_tensor(x2[:, :, :], y_sb[:, :, :], x_res[:, :, :], ALU.add).then_inc(x2_ready, 1)
                if name == "x2stat":
                    dve.wait_ge(x2_ready, it)
                    layer_stats("x2", x2, x2_stats, x2_mv, it)
                if name == "x2n":
                    normalise("x2", x2_n, x2, x2_rstd, x2_norm, it)
                if name == "route":
                    dve.wait_ge(misc_written, misc_at(it, (s_of(it, "lg"), "lg", 0)) + 1)
                    lg = misc_tok[:, :, 0:E]
                    nc.vector.reduce_max(lmax[:, :], lg, AX_X).then_inc(lmax_ready, 1)
                    dve.wait_ge(lmax_ready, it)
                    nc.vector.tensor_tensor(logit[:, :, :], lg, lmax[:, :].unsqueeze(2).to_broadcast([P, TT, E]),
                                            ALU.subtract).then_inc(misc_read, 1)
                if name == "prob":
                    r0 = it * ROUTE_STEPS - ROUTE_STEPS
                    dve.wait_ge(expo_ready, it)
                    nc.vector.reduce_sum(esum[:, :], expo[:, :, :], AX_X).then_inc(route_step, 1)
                    dve.wait_ge(route_step, r0 + 1)
                    nc.vector.reciprocal(erec[:, :], esum[:, :]).then_inc(route_step, 1)
                    dve.wait_ge(route_step, r0 + 2)
                    nc.vector.tensor_tensor(prob[:, :, :], expo[:, :, :], erec[:, :].unsqueeze(2).to_broadcast([P, TT, E]),
                                            ALU.mult).then_inc(route_step, 1)
                if name == "above":
                    r0 = it * ROUTE_STEPS - ROUTE_STEPS
                    big = [P, TT, E, E]
                    dve.wait_ge(route_step, r0 + 3)
                    other = prob[:, :, :].unsqueeze(2).to_broadcast(big)
                    own = prob[:, :, :].unsqueeze(3).to_broadcast(big)
                    nc.vector.tensor_tensor(equal[:, :, :, :], other, own, ALU.is_equal).then_inc(route_step, 1)
                    nc.vector.tensor_tensor(above[:, :, :, :], other, own, ALU.is_gt).then_inc(route_step, 1)
                    dve.wait_ge(route_step, r0 + 4)
                    nc.vector.tensor_tensor(equal[:, :, :, :], equal[:, :, :, :],
                                            earlier[:, :, :].unsqueeze(1).to_broadcast(big), ALU.mult).then_inc(route_step, 1)
                if name == "rank":
                    r0 = it * ROUTE_STEPS - ROUTE_STEPS
                    dve.wait_ge(route_step, r0 + 6)
                    nc.vector.tensor_tensor(above[:, :, :, :], above[:, :, :, :], equal[:, :, :, :],
                                            ALU.add).then_inc(route_step, 1)
                    dve.wait_ge(route_step, r0 + 7)
                    nc.vector.reduce_sum(rank[:, :, :], above[:, :, :, :], AX_X).then_inc(route_step, 1)
                    dve.wait_ge(route_step, r0 + 8)
                    nc.vector.scalar_tensor_tensor(coef[:, :, :], rank[:, :, :], 1.5, prob[:, :, :], ALU.is_lt,
                                                   ALU.mult).then_inc(coef_ready, 1)
                if name == "g":
                    dve.wait_ge(tanh_ready, it * MB + (a + 1 - MB))
                    need(dve, up_read, it * MB + ((max(a - 1, 0) if last(it) else a) - MB))
                    nc.vector.scalar_tensor_tensor(silu_of(it, a)[:, :], tanh_sb[:, :], 1.0, gate_of(it, a)[:, :], ALU.add,
                                                   ALU.mult).then_inc(gate_read, 1)
                if name == "u":
                    dve.wait_ge(up_written, it * MB + (a + 1 - MB))
                    dve.wait_ge(gate_read, it * GATE_USES + (a + 1 - GATE_USES))
                    nc.vector.scalar_tensor_tensor(hidden[:, a, :], silu_of(it, a)[:, :], 0.5, up_of(it, a)[:, :], ALU.mult,
                                                   ALU.mult).then_inc(up_read, 1)
                if name == "c" and last(it):
                    dve.wait_ge(misc_written, misc_at(it, (s, "c", a)) + 1)
                    dve.wait_ge(up_read, it * MB + (a + 1 - MB))
                    nc.vector.tensor_tensor(hidden[:, a, :], hidden[:, a, :], misc[:, :], ALU.mult).then_inc(misc_read, 1)
                if name == "fin":
                    need(dve, out_ready, it - 1)
                    dve.wait_ge(down_written, it)
                    nc.vector.tensor_tensor(ffn_sb[:, :, :], down_of(it)[:, :].rearrange("p (t c) -> p t c", t=TT),
                                            over_tiles(gate_b[:, it - 1, :]), ALU.mult).then_inc(gate_read, 1)
                    if last(it):
                        dve.wait_ge(gate_read, it * GATE_USES)
                        dve.wait_ge(stored, it * 16 - 16)
                        nc.vector.tensor_tensor(out_sb[:, :, :], ffn_sb[:, :, :], x2[:, :, :], ALU.add).then_inc(out_ready, 1)

            walk(dve, "dve", run)

        @block.tensor
        def _(pe):
            def condition():
                pe.wait_ge(const_done, 1)
                pe.wait_ge(ct_step, 2)
                nc.tensor.transpose(pv_bank[:, 0:B], cond_s[:, :], ident[0:B, 0:B]).then_inc(cond_mm, 1)
                pe.wait_ge(ct_step, 3)
                for i, j in enumerate((0, 3, 1, 4)):
                    final = nc.tensor.matmul(up_bank[:, B * i:B * (i + 1)], wmod_sb[:, C * j:C * (j + 1)], cond_T[:, :],
                                            start=True, stop=True)
                final.then_inc(cond_mm, 1)

            def gates(i):
                pe.wait_ge(ct_step, 6)
                half = B // 2
                for b in range(half):
                    last_mm = nc.tensor.matmul((s1_bank, s2_bank)[i // 2][i % 2][:, C * b:C * (b + 1)],
                                               cond_rep[:, half * (i % 2) + b, :],
                                               wmod_sb[:, C * (2, 5)[i // 2]:C * ((2, 5)[i // 2] + 1)],
                                               start=True, stop=True)
                last_mm.then_inc(cond_mm, 1)

            def take_misc(it, task):
                need(pe, misc_read, misc_at(it, task))

            def transposes(dst, src, idn):
                for t in range(TT):
                    final = nc.tensor.transpose(dst[:, P * t:P * (t + 1)], src(t), idn[:, :])
                return final

            def run(it, s, name, a):
                if name == "cond":
                    condition()
                if name == "gates":
                    gates(a)
                if name == "v" and isinstance(it, int) and it == 0:
                    pe.wait_ge(ffn_in, 16 * FFN_DMAS)
                    pe.wait_ge(const_step, 3 + PARTS)
                if name == "q" and isinstance(it, int):
                    pe.wait_ge(qkv_in, 16 * QKV_DMAS)
                if name == "xt":
                    pe.wait_ge(x_norm, it + 2)
                    take_misc(it, (s, "xt", 0))
                    transposes(misc, lambda t: x_n[:, t, :], ident).then_inc(misc_written, 1)
                if name in ("q", "k"):
                    take_misc(it, (s, name, 0))
                    nc.tensor.matmul(misc[:, :], (wq if name == "q" else wk)[:, :], h1T[:, :],
                                     start=True, stop=True).then_inc(misc_written, 1)
                if name == "v":
                    take_misc(it, (s, "v", 0))
                    for t in range(TT):
                        final = nc.tensor.matmul(misc_tok[:, t, :], h1T[:, P * t:P * (t + 1)], wv[:, :],
                                                start=True, stop=True)
                    final.then_inc(misc_written, 1)
                if name == "s1":
                    u = U1 * s + a
                    h0, nh, qt = S1_UNITS[a]
                    if a == 0:
                        if isinstance(it, int) and it == 0 and s == 0:
                            pe.wait_ge(gates_read, 4)
                        pe.wait_ge(stacked[s], it * (16 * Q_DMAS) + 16 * Q_DMAS)
                    need(pe, s1_reduced, it * (G * U1) + (u - 1))
                    w = P * (qt + 1)
                    dst = s1_bank[u % 2]
                    for i in range(nh):
                        h = GH * s + h0 + i
                        nc.tensor.matmul(dst[:, w * i:w * (i + 1)], q_stack[0:KROWS, h, P * qt:P * (qt + 1)],
                                         k_stack[0:KROWS, h, 0:w], start=True, stop=False)
                        final = nc.tensor.matmul(dst[:, w * (i + 1) - P:w * (i + 1)], ident_bf[:, :], causal[:, :],
                                                start=False, stop=True)
                    final.then_inc(s1_written, 1)
                if name == "s2":
                    u = U2 * (s - 1) + a
                    g = (s - 1) % G
                    if a == 0:
                        pe.wait_ge(max_landed, it * (16 * G) + 16 * s)
                    need(pe, exp_done, it * (G * U2) + (u - 1))
                    dst, at = s2_bank[u % 2], 0
                    for h, j in S2_UNITS[a]:
                        w = T - P * j
                        hh = GH * g + h
                        final = nc.tensor.matmul(dst[:, at:at + w], k_stack[0:MROWS, hh, P * j:P * (j + 1)],
                                                q_stack[0:MROWS, hh, P * j:T], start=True, stop=True)
                        at += w
                    final.then_inc(s2_written, 1)
                if name == "pv":
                    n = s - 1 if a == 0 else s - 2
                    g = n % G
                    j, units = PV_ORDER[a]
                    pe.wait_ge(probs_ready, it * (G * U2) + (U2 * n + units))
                    if a == 0:
                        need(pe, u_ready, it * G + (s - 1))
                        pe.wait_ge(v_ready, it + (1 if s > 0 else 0))
                    for h in range(GH):
                        final = nc.tensor.matmul(pv_bank[VC * h:VC * (h + 1), P * j:T], v_aug[:, j, GH * g + h, :],
                                                probs[g % 2][:, h, P_AT[j]:P_AT[j] + T - P * j],
                                                start=(a == 0), stop=(a == len(PV_ORDER) - 1))
                    if a == len(PV_ORDER) - 1:
                        final.then_inc(pv_done, 1)
                if name == "max":
                    need_all(pe, (const_done, 1), (max_step, it * (G * 4) + 4 * (s + 1)), (misc_read, misc_at(it, (s, "max", 0))))
                    nc.tensor.transpose(misc_bf[0:PARTS * GH * TT, 0:P],
                                        max_parts[:, :, :].rearrange("p a b -> p (a b)"),
                                        ident_bf[:, :]).then_inc(misc_written, 1)
                if name == "o":
                    pe.wait_ge(u_ready, it * G + (s - 1))
                    take_misc(it, (s, "o", 0))
                    transposes(misc, lambda t: u_sb[:, P * t:P * (t + 1)], ident).then_inc(misc_written, 1)
                if name == "ot":
                    take_misc(it, (s, "ot", 0))
                    transposes(misc, lambda t: o_tok[:, t, :], ident).then_inc(misc_written, 1)
                if name == "y":
                    take_misc(it, (s, "y", 0))
                    for t in range(TT):
                        final = nc.tensor.matmul(misc_tok[:, t, :], oT[:, P * t:P * (t + 1)], wo[:, :],
                                                start=True, stop=True)
                    final.then_inc(misc_written, 1)
                if name == "x2t":
                    pe.wait_ge(x2_norm, it)
                    take_misc(it, (s, "x2t", 0))
                    transposes(misc, lambda t: x2_n[:, t, :], ident).then_inc(misc_written, 1)
                if name == "lg":
                    take_misc(it, (s, "lg", 0))
                    for t in range(TT):
                        final = nc.tensor.matmul(misc_tok[:, t, :], h2T[:, P * t:P * (t + 1)], w_router[:, :],
                                                start=True, stop=True)
                    final.then_inc(misc_written, 1)
                if name == "ct":
                    pe.wait_ge(coef_split, it)
                    take_misc(it, (s, "ct", 0))
                    transposes(misc_bf, lambda t: coef_parts[:, t, :], ident_bf).then_inc(misc_written, 1)
                if name == "g":
                    if a == 0:
                        pe.wait_ge(misc_read, misc_at(it, (s_of(it, "x2t"), "x2t", 0)) + 1)
                    if not last(it):
                        need(pe, gate_read, it * GATE_USES + (a - GATE_USES))
                    elif a == 1:
                        pe.wait_ge(s1_reduced, it * (G * U1))
                    else:
                        pe.wait_ge(gate_read, it * GATE_USES + (max(a - 1, 0) - GATE_USES))
                    nc.tensor.matmul(gate_of(it, a)[:, :], wg[:, P * a:P * (a + 1)], h2T[:, :], start=True,
                                     stop=True).then_inc(gate_written, 1)
                if name == "u":
                    if not last(it):
                        need(pe, up_read, it * MB + (a - MB))
                    elif a == 1:
                        pe.wait_ge(s1_reduced, it * (G * U1))
                    else:
                        pe.wait_ge(up_read, it * MB + (max(a - 1, 0) - MB))
                    nc.tensor.matmul(up_of(it, a)[:, :], wu[:, P * a:P * (a + 1)], h2T[:, :], start=True,
                                     stop=True).then_inc(up_written, 1)
                if name == "c":
                    take_misc(it, (s, "c", a))
                    nc.tensor.matmul(misc[:, :], pick[:, a, :, :].rearrange("p a b -> p (a b)"), coef_T[:, :],
                                     start=True, stop=True).then_inc(misc_written, 1)
                if name == "down":
                    m = (a + FB) % MB
                    if a == 0:
                        pe.wait_ge(up_read, it * MB)
                        pe.wait_ge(gate_read, it * GATE_USES - 1)
                        if last(it):
                            pe.wait_ge(exp_done, it * (G * U2))
                        nc.tensor.matmul(down_of(it)[:, :], zero_row[:, 0:P], zero_row[:, :], start=True, stop=False)
                    elif last(it):
                        pe.wait_ge(misc_read, misc_at(it, (s, "c", a - 1)) + 1)
                    else:
                        pe.wait_ge(weighted, it * FB + (a - FB))
                    for t in range(TT):
                        last_mm = nc.tensor.matmul(down_of(it)[:, P * t:P * (t + 1)], hidden[:, m, P * t:P * (t + 1)],
                                                   wd[:, m, :], start=False, stop=(a == MB - 1 and t == TT - 1))
                    if a == MB - 1:
                        last_mm.then_inc(down_written, 1)

            walk(pe, "pe", run)


_INS = ["L0_attn_x", "L0_attn_Wq", "L0_attn_bq", "L0_attn_Wk", "L0_attn_bk", "L0_attn_Wv", "L0_attn_bv",
        "L0_attn_Wo", "L0_attn_bo", "L0_attn_gamma", "L0_attn_beta", "L0_ffn_router", "L0_ffn_experts_gate",
        "L0_ffn_experts_up", "L0_ffn_experts_down", "L0_ffn_shared_gate", "L0_ffn_shared_up",
        "L0_ffn_shared_down", "L0_c", "L0_wmod"]


def kernel(**inputs):
    import numpy as np
    import concourse.bacc as bacc
    from concourse.bass_utils import run_bass_kernel_spmd

    nc = bacc.Bacc("TRN2", target_bir_lowering=False, num_devices=1)
    arrays, args = {}, []
    for name in _INS:
        a = np.ascontiguousarray(inputs[name])
        arrays[f"in_{name}"] = a
        args.append(nc.dram_tensor(f"in_{name}", a.shape, mybir.dt.from_np(a.dtype), kind="ExternalInput").ap())
    args.append(nc.dram_tensor("out_x", (B, T, C), F32, kind="ExternalOutput").ap())
    block_kernel(nc, *args)
    r = run_bass_kernel_spmd(nc, [arrays], core_ids=[0])
    return r.results[0]["out_x"]
```
